# Optimizing a Trainium2 kernel written in Bass

```python
import numpy as np
import jax
import jax.numpy as jnp

def _softmax(x, axis=-1):
    return jax.nn.softmax(x, axis=axis)

def _gelu(x):
    return jax.nn.gelu(x, approximate=True)

def _silu(x):
    return jax.nn.silu(x)

def _sigmoid(x):
    return jax.nn.sigmoid(x)

def _layernorm(x, axis=-1, eps=1e-05):
    m = jnp.mean(x, axis=axis, keepdims=True)
    v = jnp.var(x, axis=axis, keepdims=True)
    return (x - m) / jnp.sqrt(v + eps)

def _scatter_add(tgt, idx, src, axis=0):
    return tgt.at[idx].add(src)

def _segment_sum(src, seg, n):
    return jax.ops.segment_sum(src, seg, n)
kernel_name = 'mk_decoder_postln_d1_seqx_r8_ecb255'

def setup_inputs(seed: int=0):
    np.random.seed(seed)
    _w = jnp.asarray

    def _rec_inputs():
        import jax
        import jax.numpy as jnp
        _rk = jax.random.key(seed)
        x = 0.0003765 + 1 * jax.random.normal(jax.random.fold_in(_rk, 1), (8, 128, 256), jnp.float32)
        _lenS = 128 - jax.random.randint(jax.random.fold_in(_rk, 7), (8,), 0, max(1, 128 // 4) + 1, jnp.int32)
        _lenS2 = 128 - jax.random.randint(jax.random.fold_in(_rk, 8), (8,), 0, max(1, 128 // 4) + 1, jnp.int32)
        _ctx_2048P = jax.random.normal(jax.random.fold_in(_rk, 11), (8, 16, 256), jnp.float32)
        _ctx_2048c = jax.random.dirichlet(jax.random.fold_in(_rk, 511), 0.3 * jnp.ones((16,), jnp.float32), (8, 128))
        _ctx_2048t = jnp.einsum('bsk,bkd->bsd', _ctx_2048c, _ctx_2048P)
        _ctx_2048t = _ctx_2048t * jax.lax.rsqrt(jnp.mean(jnp.square(_ctx_2048t)) + 1e-12) * 0.953939
        ctx_2048 = -0.000292821 + 1.00034 * (_ctx_2048t + 0.3 * jax.random.normal(jax.random.fold_in(_rk, 611), (8, 128, 256), jnp.float32))
        return (x, ctx_2048)
    x, ctx_2048 = _rec_inputs()

    def _L0_attn_setup():
        import jax, jax.numpy as jnp
        import numpy as np
        B, S, D = (2, 256, 256)
        H, KVH, DH = (16, 4, 128)
        WIN = 128
        THETA = 10000.0

        def _rotate_half(t):
            half = t.shape[-1] // 2
            return jnp.concatenate([-t[..., half:], t[..., :half]], axis=-1)

        def _rope_tables(seq_len, head_dim, theta, dtype):
            inv_freq = 1.0 / theta ** (jnp.arange(0, head_dim, 2, dtype=jnp.float32) / head_dim)
            freqs = jnp.arange(seq_len, dtype=jnp.float32)[:, None] * inv_freq[None, :]
            cos = jnp.repeat(jnp.cos(freqs), 2, axis=-1).astype(dtype)
            sin = jnp.repeat(jnp.sin(freqs), 2, axis=-1).astype(dtype)
            return (cos[None, :, None, :], sin[None, :, None, :])
        key = jax.random.key(seed)
        ks = jax.random.split(key, 5)
        return {'x': jax.random.normal(ks[0], (B, S, D), dtype=jnp.float32), 'Wq': jax.random.normal(ks[1], (H * DH, D), dtype=jnp.float32) * 0.02, 'Wk': jax.random.normal(ks[2], (KVH * DH, D), dtype=jnp.float32) * 0.02, 'Wv': jax.random.normal(ks[3], (KVH * DH, D), dtype=jnp.float32) * 0.02, 'Wo': jax.random.normal(ks[4], (D, H * DH), dtype=jnp.float32) * 0.02}
    _L0_attn_all = _L0_attn_setup()
    _L0_attn_in = {k: v for k, v in _L0_attn_all.items() if k in ('Wq', 'Wk', 'Wv', 'Wo')}
    del _L0_attn_all

    def _L0_xattn_setup():
        import jax, jax.numpy as jnp
        import numpy as np
        key = jax.random.key(seed)
        k1, k2, k3, k4, k5 = jax.random.split(key, 5)
        B, D_MODEL, L = (2, 128, 256)
        HEAD_DIM = 8
        H = D_MODEL // HEAD_DIM
        return {'k': jax.random.normal(k1, (B, D_MODEL, L), dtype=jnp.float32), 'v': jax.random.normal(k2, (B, D_MODEL, L), dtype=jnp.float32), 'q': jax.random.normal(k3, (B, D_MODEL, L), dtype=jnp.float32), 'ssm_kernel': jax.random.normal(k4, (H, L), dtype=jnp.float32), 'D': jax.random.normal(k5, (H,), dtype=jnp.float32), 'head_dim': HEAD_DIM}
    _L0_xattn_all = _L0_xattn_setup()
    _L0_xattn_in = {k: v for k, v in _L0_xattn_all.items() if k in ('ssm_kernel', 'D')}
    del _L0_xattn_all

    def _L0_ffn_setup():
        import jax, jax.numpy as jnp
        import numpy as np
        import math
        N_EMBD = 256
        N_HEAD = 16
        HEAD_DIM = N_EMBD // N_HEAD
        B, T = (2, 256)
        key = jax.random.key(seed)
        k1, k2, k3 = jax.random.split(key, 3)
        x = jax.random.normal(k1, (B, T, N_EMBD), dtype=jnp.float32)
        W_gate = jax.random.normal(k2, (N_HEAD, N_EMBD), dtype=jnp.float32) * 0.02
        W_qkv = jax.random.normal(k3, (3 * N_EMBD, N_EMBD), dtype=jnp.float32) * 0.02
        return {'x': x, 'W_gate': W_gate, 'W_qkv': W_qkv}
    _L0_ffn_all = _L0_ffn_setup()
    _L0_ffn_in = {k: v for k, v in _L0_ffn_all.items() if k in ('W_gate', 'W_qkv')}
    del _L0_ffn_all
    return {'x': x, 'ctx_2048': ctx_2048, 'L0_attn_Wq': _L0_attn_in['Wq'], 'L0_attn_Wk': _L0_attn_in['Wk'], 'L0_attn_Wv': _L0_attn_in['Wv'], 'L0_attn_Wo': _L0_attn_in['Wo'], 'L0_xattn_ssm_kernel': _L0_xattn_in['ssm_kernel'], 'L0_xattn_D': _L0_xattn_in['D'], 'L0_ffn_W_gate': _L0_ffn_in['W_gate'], 'L0_ffn_W_qkv': _L0_ffn_in['W_qkv']}

def reference(x, ctx_2048, L0_attn_Wq, L0_attn_Wk, L0_attn_Wv, L0_attn_Wo, L0_xattn_ssm_kernel, L0_xattn_D, L0_ffn_W_gate, L0_ffn_W_qkv):
    import jax
    import jax.numpy as jnp

    def _L0_attn_ref(x, Wq, Wk, Wv, Wo):
        import jax, jax.numpy as jnp
        import numpy as np
        B, S, D = (2, 256, 256)
        H, KVH, DH = (16, 4, 128)
        WIN = 128
        THETA = 10000.0

        def _rotate_half(t):
            half = t.shape[-1] // 2
            return jnp.concatenate([-t[..., half:], t[..., :half]], axis=-1)

        def _rope_tables(seq_len, head_dim, theta, dtype):
            inv_freq = 1.0 / theta ** (jnp.arange(0, head_dim, 2, dtype=jnp.float32) / head_dim)
            freqs = jnp.arange(seq_len, dtype=jnp.float32)[:, None] * inv_freq[None, :]
            cos = jnp.repeat(jnp.cos(freqs), 2, axis=-1).astype(dtype)
            sin = jnp.repeat(jnp.sin(freqs), 2, axis=-1).astype(dtype)
            return (cos[None, :, None, :], sin[None, :, None, :])
        b, s, _ = x.shape
        q = (x @ Wq.T).reshape(b, s, H, DH)
        k = (x @ Wk.T).reshape(b, s, KVH, DH)
        v = (x @ Wv.T).reshape(b, s, KVH, DH)
        cos, sin = _rope_tables(s, DH, THETA, x.dtype)
        q = q * cos + _rotate_half(q) * sin
        k = k * cos + _rotate_half(k) * sin
        groups = H // KVH
        k = jnp.repeat(k, groups, axis=2)
        v = jnp.repeat(v, groups, axis=2)
        q = q.transpose(0, 2, 1, 3)
        k = k.transpose(0, 2, 1, 3)
        v = v.transpose(0, 2, 1, 3)
        scale = DH ** (-0.5)
        scores = jnp.einsum('bhqd,bhkd->bhqk', q, k) * scale
        iq = jnp.arange(s)[:, None]
        ik = jnp.arange(s)[None, :]
        mask = iq >= ik - WIN
        scores = jnp.where(mask[None, None, :, :], scores, jnp.float32(-jnp.inf).astype(scores.dtype))
        attn = jax.nn.softmax(scores, axis=-1)
        out = jnp.einsum('bhqk,bhkd->bhqd', attn, v)
        out = out.transpose(0, 2, 1, 3).reshape(b, s, H * DH)
        return out @ Wo.T

    def _L0_xattn_ref(k, v, q, ssm_kernel, D, head_dim):
        import jax, jax.numpy as jnp
        import numpy as np
        B, HD, L = k.shape
        H = HD // head_dim
        fft_size = 2 * L
        k_ = k.reshape(B, H, head_dim, L)
        v_ = v.reshape(B, H, head_dim, L)
        q_ = q.reshape(B, H, head_dim, L)
        kv = jnp.einsum('bhil,bhjl->bijhl', k_, v_)
        kv_f = jnp.fft.rfft(kv, n=fft_size)
        kernel_f = jnp.fft.rfft(ssm_kernel, n=fft_size)
        y = jnp.fft.irfft(kv_f * kernel_f, n=fft_size)[..., :L]
        out = y + kv * D[None, None, None, :, None]
        out = jnp.einsum('bijhl,bhil->bjhl', out, q_)
        out = jnp.transpose(out, (0, 2, 1, 3)).reshape(B, H * head_dim, L)
        return out.astype(k.dtype)

    def _L0_ffn_ref(x, W_gate, W_qkv):
        import jax, jax.numpy as jnp
        import numpy as np
        import math
        N_EMBD = 256
        N_HEAD = 16
        HEAD_DIM = N_EMBD // N_HEAD
        B, T = (2, 256)
        Bb, Tt, C = x.shape
        H, hd = (N_HEAD, HEAD_DIM)
        gating = jax.nn.softmax(x @ W_gate.T, axis=-1)
        idx = jnp.argmax(gating, axis=-1)
        indicator = jax.nn.one_hot(idx, H, dtype=gating.dtype)
        top1_val = jnp.max(gating, axis=-1, keepdims=True)
        gating_top1 = indicator * top1_val
        qkv = x @ W_qkv.T
        q, k, v = jnp.split(qkv, 3, axis=-1)
        k = k.reshape(Bb, Tt, H, hd)
        v = v.reshape(Bb, Tt, H, hd)
        k_shared = jnp.einsum('bth,bthd->btd', indicator, k)
        v_shared = jnp.einsum('bth,bthd->btd', gating_top1, v)
        q = q.reshape(Bb, Tt, H, hd).transpose(0, 2, 1, 3)
        att = jnp.einsum('bhqd,bkd->bhqk', q, k_shared) * (1.0 / math.sqrt(hd))
        causal = jnp.tril(jnp.ones((Tt, Tt), dtype=bool))
        att = jnp.where(causal[None, None, :, :], att, -jnp.inf)
        att = jax.nn.softmax(att, axis=-1)
        y = jnp.einsum('bhqk,bkd->bhqd', att, v_shared)
        y = y.transpose(0, 2, 1, 3).reshape(Bb, Tt, C)
        return y
    x = _layernorm(x + _L0_attn_ref(x, L0_attn_Wq, L0_attn_Wk, L0_attn_Wv, L0_attn_Wo), axis=-1)
    x = _layernorm(x + _L0_xattn_ref(ctx_2048, ctx_2048, x, L0_xattn_ssm_kernel, L0_xattn_D, 8), axis=-1)
    x = _layernorm(x + _L0_ffn_ref(x, L0_ffn_W_gate, L0_ffn_W_qkv), axis=-1)
    return x

_drawn_inputs = setup_inputs


def setup_inputs(seed=0):
    import zlib

    import numpy as np

    out = dict(_drawn_inputs(seed))
    spreads = {}
    factors = {'L0_attn_Wq': 8.0, 'L0_attn_Wk': 8.0, 'L0_ffn_W_gate': 7.076, 'L0_ffn_W_qkv': 7.053}
    for name, (base, spread) in spreads.items():
        noise = np.random.default_rng([zlib.crc32(name.encode()), seed]).standard_normal(out[name].shape)
        drawn = base * np.exp(spread * noise) if base else spread * noise
        out[name] = jnp.asarray(drawn.astype(out[name].dtype))
    for name, factor in factors.items():
        out[name] = (out[name] * factor).astype(out[name].dtype)
    return out
```

```python
import concourse.bass as bass
from concourse import mybir
from contextlib import ExitStack

FP32 = mybir.dt.float32
BF16 = mybir.dt.bfloat16
FP32R = mybir.dt.float32r
ALU = mybir.AluOpType
ACT = mybir.ActivationFunctionType
AX = mybir.AxisListType

P = 128
NB = 8
D = 256
C = D // P
NG = 4
HG = 4
NH = NG * HG
NS = 2
BH = NB // NS
TOK = BH * P
UNITS = NG * NS
XH = 16
HD = 8
NPAIR = HD * (HD + 1) // 2
PAIR_AT = [sum(HD - e for e in range(d)) for d in range(HD)]
FH = 16
FD = 16
FB = P // FD
EPS = 1e-5
CONV = 4

COLS = ["K", "Q0", "Q1", "Q2", "Q3", "V"]
FRONT = ["K", "Q0", "Q1", "Q2", "Q3", "C0", "V"]
BODY = ["K", "Q0", "Q1", "Q2", "Q3", "C1", "C2", "C3", "C0", "V"]
LAST = ["C1", "C2", "C3"]
ROPED = ["K", "Q0", "Q1", "Q2", "Q3"]


def decoder_kernel(nc, xt_d, x_d, wqkv_d, wo_d, toep_d, dcoef_d, ctx_d, wf_d, cos_d, sin_d, ident_d,
                   anti_d, causal_d, blocks_d, ties_d, out_d):
    ctx = ExitStack()
    with ctx:
        def sb(name, shape, dt=FP32):
            return ctx.enter_context(nc.sbuf_tensor(name, shape, dt))

        def sem(name):
            return ctx.enter_context(nc.semaphore(name))

        x_raw = sb("x_raw", [P, C, TOK])
        x_hi = sb("x_hi", [P, NS, C, TOK], FP32R)
        x_lo = sb("x_lo", [P, NS, C, TOK], FP32R)
        x = sb("x", [P, NB, D])
        w_raw = sb("w_raw", [P, C, 6 * P])
        w_hi = sb("w_hi", [P, C, 6 * P], FP32R)
        w_lo = sb("w_lo", [P, C, 6 * P], FP32R)
        wo_raw = sb("wo_raw", [P, HG, D])
        wo_hi = sb("wo_hi", [P, NH, D], FP32R)
        wo_lo = sb("wo_lo", [P, NH, D], FP32R)
        toep = sb("toep", [P, 2, 2, D])
        dcoef = sb("dcoef", [P, XH])
        ctxT = sb("ctxT", [P, C, XH * NB, HD])
        kv = sb("kv", [P, 2, C, 2 * NB, NPAIR])
        y36 = sb("y36", [P, NB, C, XH, NPAIR])
        cos = sb("cos", [P, P])
        sin = sb("sin", [P, P])
        ident = sb("ident", [P, P])
        anti = sb("anti", [P, P])
        identb = sb("identb", [P, P], BF16)
        causal_raw = sb("causal_raw", [P, P])
        causal = sb("causal", [P, P], BF16)
        blocks = sb("blocks", [P, FB])
        ties = sb("ties", [P, FH])
        half_pow = sb("half_pow", [P, BH])
        q_rope = sb("q_rope", [P, 2, HG, TOK])
        k_rope = sb("k_rope", [P, 2, TOK])
        v_tok = sb("v_tok", [P, 2, TOK])
        rot = sb("rot", [P, 2, TOK])
        t_cos = sb("t_cos", [P, 2, TOK])
        t_sin = sb("t_sin", [P, 2, TOK])
        neg_max = sb("neg_max", [P, 2, HG])
        den = sb("den", [P, 2, HG])
        rden = sb("rden", [P, 2, HG])
        prob = sb("prob", [P, 2, HG * P])
        probT = sb("probT", [P, 2, HG * P])
        head_hi = sb("head_hi", [P, 2, HG * P], FP32R)
        head_lo = sb("head_lo", [P, 2, HG * P], FP32R)
        stats = sb("stats", [P, BH, 6])
        mean_var1 = sb("mean_var1", [P, NB, 2])
        rstd1 = sb("rstd1", [P, NB])
        mean_var = sb("mean_var", [P, 2])
        var_eps = sb("var_eps", [P, BH])
        rstd = sb("rstd", [P, 1])
        carrier = sb("carrier", [P, 1])
        prod = q_rope[:, :, :, :].rearrange("p n h t -> p n (h t)").rearrange(
            "p n (a j i) -> p n a j i", j=HD, i=HD)
        kblock = ctxT[:, :, :, :].rearrange("p c a i -> p c (a i)").rearrange("p c (h k) -> p c h k", k=P)
        wf = sb("wf", [P, C, 3 * D + FH])
        qmix = rot[:, :, 0:D]
        mixT = t_cos[:, :, 0:D]
        x1 = v_tok[:, :, 0:D]
        x2 = v_tok[:, :, D:2 * D]
        x2T = k_rope[:, :, 0:D]
        qf = k_rope[:, :, D:2 * D]
        gate = sb("gate", [P, FH])
        gexp = sb("gexp", [P, FH])
        gtop = sb("gtop", [P, 1])
        gneg = sb("gneg", [P, 1])
        gsum = sb("gsum", [P, 1])
        gprob = sb("gprob", [P, 1])
        gscore = sb("gscore", [P, FH])
        gbest = sb("gbest", [P, 1])
        chosen = sb("chosen", [P, FH])
        kv_masked = sb("kv_masked", [P, 2, FH, FD])
        kv_shared = sb("kv_shared", [P, 2, FD])
        krep = sb("krep", [P, FB, FD])
        ksT = sb("ksT", [P, P])
        vext = sb("vext", [P, 2, FD + 1])
        yden = sb("yden", [P, FH])
        ynorm = sb("ynorm", [P, FH, FD])

        bank = [ctx.enter_context(nc.psum_tensor(f"bank{i}", [P, 512], FP32)) for i in range(8)]
        proj_bank = [bank[0], bank[1]]
        score_bank = [bank[2], bank[3]]
        probT_bank, headT_bank = bank[4], bank[5]
        acc_bank = [bank[6], bank[7]]
        fscore_bank = [bank[0], bank[1]]
        fprobT_bank = [bank[2], bank[3]]
        mix_bank, kvf_bank, tf_bank, y_bank = bank[4], bank[5], bank[6], bank[7]

        in_xt = sem("in_xt")
        x_hi_done = sem("x_hi_done")
        x_lo_done = sem("x_lo_done")
        w_hi_done = sem("w_hi_done")
        w_lo_done = sem("w_lo_done")
        wo_hi_done = sem("wo_hi_done")
        wo_lo_done = sem("wo_lo_done")
        in_w = sem("in_w")
        in_wo = sem("in_wo")
        in_trig = sem("in_trig")
        in_ident = sem("in_ident")
        in_toep = [sem("in_toep0"), sem("in_toep1")]
        in_skip = sem("in_skip")
        in_ctx = sem("in_ctx")
        in_x = sem("in_x")
        in_ffn = sem("in_ffn")
        const_set = sem("const_set")
        mask_done = sem("mask_done")
        toep_done = sem("toep_done")
        proj_done = sem("proj_done")
        rot_done = sem("rot_done")
        cos_done = sem("cos_done")
        sin_done = sem("sin_done")
        rope_done = sem("rope_done")
        v_done = sem("v_done")
        conv_done = sem("conv_done")
        kv_done = sem("kv_done")
        scores_done = sem("scores_done")
        max_done = sem("max_done")
        exp_done = sem("exp_done")
        rden_done = sem("rden_done")
        norm_done = sem("norm_done")
        pt_done = sem("pt_done")
        ptcopy_done = sem("ptcopy_done")
        pv_done = sem("pv_done")
        head_hi_done = sem("head_hi_done")
        head_lo_done = sem("head_lo_done")
        wo_done = sem("wo_done")
        acc_done = sem("acc_done")
        ln1 = [sem(f"ln1_{n}") for n in ("stats", "aggr", "eps", "rstd", "out")]
        ln2 = [sem(f"ln2_{n}") for n in ("sum", "stats", "aggr", "eps", "rstd", "out")]
        ln3 = [sem(f"ln3_{n}") for n in ("sum", "stats", "aggr", "eps", "rstd", "out")]
        x1T_done = sem("x1T_done")
        qmix_done = sem("qmix_done")
        prod_done = sem("prod_done")
        mixT_done = sem("mixT_done")
        mix_done = sem("mix_done")
        x2T_done = sem("x2T_done")
        x2copy_done = sem("x2copy_done")
        qkvf_done = sem("qkvf_done")
        qf_done = sem("qf_done")
        gtop_done = sem("gtop_done")
        gneg_done = sem("gneg_done")
        gexp_done = sem("gexp_done")
        gprob_done = sem("gprob_done")
        gscore_done = sem("gscore_done")
        gbest_done = sem("gbest_done")
        chosen_done = sem("chosen_done")
        masked_done = sem("masked_done")
        shared_done = sem("shared_done")
        krep_done = sem("krep_done")
        vext_done = sem("vext_done")
        ksT_done = sem("ksT_done")
        kscopy_done = sem("kscopy_done")
        kblock_done = sem("kblock_done")
        fscores_done = sem("fscores_done")
        fmax_done = sem("fmax_done")
        fexp_done = sem("fexp_done")
        fpt_done = sem("fpt_done")
        fptcopy_done = sem("fptcopy_done")
        y_done = sem("y_done")
        yden_done = sem("yden_done")
        ynorm_done = sem("ynorm_done")
        stored = sem("stored")

        def proj_count(u, i):
            return len(FRONT) + len(BODY) * u + i + 1

        def item_bank(i):
            return proj_bank[(len(FRONT) + i) % 2]

        def rope_count(u_next, name):
            return len(ROPED) * u_next + ROPED.index(name) + 1

        def rope_parity(j_next, name):
            return (len(ROPED) * j_next + ROPED.index(name)) % 2

        def two_back(eng, done, n, k):
            if k >= 2:
                eng.wait_ge(done, 4 * n + k - 1)

        def two_back_f(eng, done, n, j, k):
            if k >= 2:
                eng.wait_ge(done, 4 * n + k - 1)
            elif j == 1:
                eng.wait_ge(done, 4 * n)

        block = ctx.enter_context(nc.Block())

        def phase_a(eng, unit):
            with eng.Fori(0, NG - 1, 1) as v:
                unit(v, 0, True, True)
                unit(v, 1, True, True)
            unit(NG - 1, 0, True, False)
            unit(NG - 1, 1, False, False)

        def phase_b(eng, seq):
            with eng.Fori(0, NB // 2 - 1, 1) as w:
                seq(2 * w, 0, True, True)
                seq(2 * w + 1, 1, True, True)
            seq(NB - 2, 0, True, False)
            seq(NB - 1, 1, False, False)

        @block.sync
        def _(sp):
            def load_toep(u, j):
                if not (isinstance(u, int) and u <= 1):
                    sp.wait_ge(proj_done, proj_count(u - 2, BODY.index("C3")))
                sp.dma_start(toep[:, j, :, :], toep_d[:, bass.ds(2 * u, 2), :]).then_inc(in_toep[j], 16)

            sp.dma_start(x_raw[:, :, :], xt_d[:, 0, :, :]).then_inc(in_xt, 16)
            sp.dma_start(cos[:, :], cos_d).then_inc(in_trig, 16)
            sp.dma_start(sin[:, :], sin_d).then_inc(in_trig, 16)
            sp.dma_start(ctxT[:, :, :, :], ctx_d).then_inc(in_ctx, 16)
            load_toep(0, 0)
            sp.dma_start(dcoef[:, :], dcoef_d).then_inc(in_skip, 16)
            sp.dma_start(anti[:, :], anti_d).then_inc(in_skip, 16)
            sp.dma_start(ident[:, :], ident_d).then_inc(in_ident, 16)
            sp.wait_ge(x_lo_done, 1)
            sp.dma_start(x_raw[:, :, :], xt_d[:, 1, :, :]).then_inc(in_xt, 16)
            sp.dma_start(wo_raw[:, :, :], wo_d[:, 0:HG, :]).then_inc(in_wo, 16)
            load_toep(1, 1)
            sp.dma_start(x[:, :, :], x_d).then_inc(in_x, 16)
            with sp.Fori(0, NG - 1, 1) as v:
                sp.wait_ge(w_lo_done, 2 * v + 2)
                sp.dma_start(w_raw[:, :, :], wqkv_d[:, v + 1, :, :]).then_inc(in_w, 16)
                sp.wait_ge(wo_lo_done, v + 1)
                sp.dma_start(wo_raw[:, :, :], wo_d[:, bass.ds(HG * v + HG, HG), :]).then_inc(in_wo, 16)
                load_toep(2 * v + 2, 0)
                load_toep(2 * v + 3, 1)
            sp.dma_start(wf[:, :, :], wf_d).then_inc(in_ffn, 16)
            sp.dma_start(causal_raw[:, :], causal_d).then_inc(in_ffn, 16)
            sp.dma_start(blocks[:, :], blocks_d).then_inc(in_ffn, 16)
            sp.dma_start(ties[:, :], ties_d).then_inc(in_ffn, 16)

            with sp.Fori(0, NB, 1) as b:
                sp.wait_ge(ln3[5], b + 1)
                sp.dma_start(out_d[b, :, :], x[:, b, :]).then_inc(stored, 16)
            sp.wait_ge(stored, 16 * NB)

        @block.tensor
        def _(pe):
            def project(j, name, out):
                col = COLS.index(name) * P
                if name == "V":
                    for b in range(BH):
                        tok = slice(b * P, (b + 1) * P)
                        for c in range(C):
                            for n, (xp, wp) in enumerate(((x_hi, w_hi), (x_hi, w_lo), (x_lo, w_hi))):
                                last = pe.matmul(out[:, tok], xp[:, j, c, tok], wp[:, c, col:col + P],
                                                 start=(c + n == 0), stop=(c == C - 1 and n == 2))
                else:
                    for c in range(C):
                        for n, (wp, xp) in enumerate(((w_hi, x_hi), (w_hi, x_lo), (w_lo, x_hi))):
                            last = pe.matmul(out[:, :], wp[:, c, col:col + P], xp[:, j, c, :],
                                             start=(c + n == 0), stop=(c == C - 1 and n == 2))
                last.then_inc(proj_done, 1)

            def conv(j, i, bank_out):
                hh, lb = i // 2, i % 2
                out = bank_out[:, 0:NB * NPAIR]
                for m in range(lb + 1):
                    tap = (lb - m) * P
                    last = pe.matmul(out, toep[:, j, hh, tap:tap + P],
                                     kv[:, j, m, hh * NB:(hh + 1) * NB, :],
                                     start=(m == 0), stop=(m == lb))
                last.then_inc(proj_done, 1)

            def scores(u, j, k):
                if k == 0:
                    pe.wait_ge(rope_done, len(ROPED) * (u + 1))
                if isinstance(u, int) and 4 * u + k < 2:
                    pass
                else:
                    pe.wait_ge(exp_done, 4 * u + k - 1)
                for h in range(HG):
                    last = pe.matmul(score_bank[k % 2][:, h * P:(h + 1) * P],
                                     q_rope[:, j, h, k * P:(k + 1) * P],
                                     k_rope[:, j, k * P:(k + 1) * P], start=True, stop=True)
                last.then_inc(scores_done, 1)

            pe.wait_ge(x_lo_done, 1)
            for n, name in enumerate(FRONT):
                if n >= 2:
                    pe.wait_ge(cos_done, n - 1)
                if name in ("K", "Q2"):
                    pe.wait_ge(w_lo_done, 1 if name == "K" else 2)
                if name == "C0":
                    pe.wait_ge(kv_done, 1)
                    pe.wait_ge(toep_done, 1)
                    conv(0, 0, proj_bank[n % 2])
                else:
                    project(0, name, proj_bank[n % 2])
            scores(0, 0, 0)
            scores(0, 0, 1)

            def bank_free(u, items, i):
                if i >= 2:
                    name, un = items[i - 2], u + 1
                else:
                    name, un = BODY[len(BODY) - 2 + i], u
                if name == "V":
                    pe.wait_ge(v_done, un + 1)
                elif name == "C0":
                    pe.wait_ge(conv_done, CONV * un + 1)
                elif name[0] == "C":
                    pe.wait_ge(conv_done, CONV * u + int(name[1]) + 1)
                else:
                    pe.wait_ge(cos_done, rope_count(un, name))

            def unit(v, j, has_next, has_more):
                u = 2 * v + j
                items = BODY if has_next else LAST

                def item(name):
                    if name not in items:
                        return
                    i = items.index(name)
                    bank_free(u, items, i)
                    if name == "C0":
                        pe.wait_ge(kv_done, u + 2)
                        pe.wait_ge(toep_done, u + 2)
                        conv(1 - j, 0, item_bank(i))
                    elif name[0] == "C":
                        conv(j, int(name[1]), item_bank(i))
                    else:
                        if name == "K" and j == 0:
                            pe.wait_ge(x_lo_done, 2)
                        if name in ("K", "Q2") and j == 1:
                            pe.wait_ge(w_lo_done, 2 * v + (3 if name == "K" else 4))
                        project(1 - j, name, item_bank(i))

                def turn(k):
                    t = 4 * u + k
                    pe.wait_ge(norm_done, t + 1)
                    if k:
                        pe.wait_ge(ptcopy_done, t)
                    for h in range(HG):
                        last = pe.transpose(probT_bank[:, h * P:(h + 1) * P],
                                            prob[:, k % 2, h * P:(h + 1) * P], ident[:, :])
                    last.then_inc(pt_done, 1)

                def values(k):
                    t = 4 * u + k
                    if k == 0:
                        pe.wait_ge(v_done, u + 1)
                    pe.wait_ge(ptcopy_done, t + 1)
                    if k:
                        pe.wait_ge(head_lo_done, t)
                    pe.matmul(headT_bank[:, :], v_tok[:, j, k * P:(k + 1) * P], probT[:, k % 2, :],
                              start=True, stop=True).then_inc(pv_done, 1)

                def output(k):
                    t = 4 * u + k
                    if k == 0:
                        pe.wait_ge(wo_lo_done, v + 1)
                    pe.wait_ge(head_lo_done, t + 1)
                    for h in range(HG):
                        for n, (hp, wp) in enumerate(((head_hi, wo_hi), (head_hi, wo_lo),
                                                      (head_lo, wo_hi))):
                            last = pe.matmul(acc_bank[k // 2][:, (k % 2) * D:(k % 2 + 1) * D],
                                             hp[:, k % 2, h * P:(h + 1) * P], wp[:, 4 * v + h, :],
                                             start=(h + n == 0), stop=(h == HG - 1 and n == 2))
                    last.then_inc(wo_done, 1)

                item("K")
                turn(0)
                item("Q0")
                values(0)
                item("Q1")
                scores(u, j, 2)
                output(0)
                item("Q2")
                turn(1)
                item("Q3")
                values(1)
                item("C1")
                scores(u, j, 3)
                output(1)
                item("C2")
                turn(2)
                item("C3")
                values(2)
                if has_next:
                    scores(u + 1, 1 - j, 0)
                output(2)
                turn(3)
                item("C0")
                item("V")
                values(3)
                if has_next:
                    scores(u + 1, 1 - j, 1)
                output(3)

            pe.wait_ge(in_ident, 16)
            phase_a(pe, unit)

            pe.wait_ge(conv_done, CONV * UNITS)
            pe.wait_ge(exp_done, 4 * UNITS)
            pe.wait_ge(acc_done, 2 * UNITS)
            pe.wait_ge(in_ffn, 64)
            pe.wait_ge(mask_done, 1)

            def x1_turn(b, j):
                pe.wait_ge(ln1[4], b + 1)
                if isinstance(b, int) and b == 0:
                    pass
                elif isinstance(b, int) and b == 1:
                    pe.wait_ge(qmix_done, b)
                else:
                    pe.wait_ge(kscopy_done, b - 1)
                for c in range(C):
                    last = pe.transpose(mix_bank[:, c * P:(c + 1) * P], x1[:, j, c * P:(c + 1) * P],
                                        ident[:, :])
                last.then_inc(x1T_done, 1)

            def mix_turn(b, j):
                pe.wait_ge(mixT_done, b + 1)
                pe.wait_ge(qmix_done, b + 2) if not (isinstance(b, int) and b == NB - 1) \
                    else pe.wait_ge(qmix_done, NB)
                for c in range(C):
                    last = pe.transpose(mix_bank[:, c * P:(c + 1) * P], mixT[:, j, c * P:(c + 1) * P],
                                        ident[:, :])
                last.then_inc(mix_done, 1)

            def x2_turn(b, j):
                pe.wait_ge(ln2[5], b + 1)
                if not (isinstance(b, int) and b == 0):
                    pe.wait_ge(qf_done, b)
                for c in range(C):
                    last = pe.transpose(tf_bank[:, c * P:(c + 1) * P], x2[:, j, c * P:(c + 1) * P],
                                        ident[:, :])
                last.then_inc(x2T_done, 1)

            def ffn_project(b, j):
                pe.wait_ge(x2copy_done, b + 1)
                if not (isinstance(b, int) and b == 0):
                    pe.wait_ge(masked_done, b)
                for n in range(C):
                    for c in range(C):
                        pe.matmul(tf_bank[:, n * P:(n + 1) * P], wf[:, c, n * P:(n + 1) * P],
                                  x2T[:, j, c * P:(c + 1) * P], start=(c == 0), stop=(c == C - 1))
                for c in range(C):
                    pe.matmul(tf_bank[:, D:D + FH], x2T[:, j, c * P:(c + 1) * P],
                              wf[:, c, 3 * D:3 * D + FH], start=(c == 0), stop=(c == C - 1))
                for c in range(C):
                    last = pe.matmul(kvf_bank[:, :], x2T[:, j, c * P:(c + 1) * P], wf[:, c, D:3 * D],
                                     start=(c == 0), stop=(c == C - 1))
                last.then_inc(qkvf_done, 1)

            def key_turn(b, j):
                pe.wait_ge(krep_done, b + 1)
                pe.wait_ge(ln2[0], b + 1)
                pe.transpose(mix_bank[:, 0:P], krep[:, :, :].rearrange("p n d -> p (n d)"),
                             ident[:, :]).then_inc(ksT_done, 1)

            def fscores(b, j, c):
                n = 4 * b + c
                if c == 0:
                    pe.wait_ge(kblock_done, b + 1)
                    pe.wait_ge(qf_done, b + 1)
                two_back_f(pe, fexp_done, b, j, c)
                out = fscore_bank[c % 2]
                pe.matmul(out[:, :], qf[:, j, (c // 2) * P:(c // 2 + 1) * P],
                          kblock[:, j, (c % 2) * 4:(c % 2) * 4 + 4, :], start=True, stop=False)
                pe.matmul(out[:, :].rearrange("p (h k) -> p h k", k=P), identb[:, :],
                          causal[:, :].unsqueeze(1).to_broadcast([P, 4, P]),
                          start=False, stop=True).then_inc(fscores_done, 1)

            def fturn(b, j, c):
                n = 4 * b + c
                pe.wait_ge(fexp_done, n + 1)
                two_back_f(pe, fptcopy_done, b, j, c)
                for h in range(4):
                    last = pe.transpose(fprobT_bank[c % 2][:, h * P:(h + 1) * P],
                                        prob[:, c % 2, h * P:(h + 1) * P], ident[:, :])
                last.then_inc(fpt_done, 1)

            def fvalues(b, j, c):
                n = 4 * b + c
                pe.wait_ge(fptcopy_done, n + 1)
                if c == 0:
                    pe.wait_ge(vext_done, b + 1)
                for h in range(4):
                    f = 4 * c + h
                    last = pe.matmul(y_bank[:, f * (FD + 1):(f + 1) * (FD + 1)],
                                     probT[:, c % 2, h * P:(h + 1) * P], vext[:, j, :],
                                     start=True, stop=True)
                last.then_inc(y_done, 1)

            x1_turn(0, 0)
            x1_turn(1, 1)
            mix_turn(0, 0)
            x2_turn(0, 0)
            ffn_project(0, 0)
            key_turn(0, 0)

            def seq(b, j, one, two):
                fscores(b, j, 0)
                if two:
                    x1_turn(b + 2, j)
                fscores(b, j, 1)
                if one:
                    mix_turn(b + 1, 1 - j)
                fturn(b, j, 0)
                fscores(b, j, 2)
                if one:
                    x2_turn(b + 1, 1 - j)
                fvalues(b, j, 0)
                fturn(b, j, 1)
                fscores(b, j, 3)
                if one:
                    ffn_project(b + 1, 1 - j)
                fvalues(b, j, 1)
                fturn(b, j, 2)
                fvalues(b, j, 2)
                if one:
                    key_turn(b + 1, 1 - j)
                fturn(b, j, 3)
                fvalues(b, j, 3)

            phase_b(pe, seq)

        @block.scalar
        def _(act):
            act.dma_start(w_raw[:, :, :], wqkv_d[:, 0, :, :]).then_inc(in_w, 16)

            def split_w(g, part, uses):
                if part == 0:
                    act.wait_ge(in_w, 16 * g + 16)
                if uses is not None:
                    act.wait_ge(proj_done, uses)
                cols = slice(part * 3 * P, (part + 1) * 3 * P)
                act.copy(w_hi[:, :, cols], w_raw[:, :, cols]).then_inc(w_hi_done, 1)

            def split_wo(g):
                act.wait_ge(in_wo, 16 * g + 16)
                act.copy(wo_hi[:, bass.ds(HG * g, HG), :], wo_raw[:, :, :]).then_inc(wo_hi_done, 1)

            act.wait_ge(in_xt, 16)
            act.copy(x_hi[:, 0, :, :], x_raw[:, :, :]).then_inc(x_hi_done, 1)
            split_w(0, 0, None)
            split_w(0, 1, None)

            def rotate(u_next, j_next, name, bank_in, count):
                r, par = rope_count(u_next, name), rope_parity(j_next, name)
                act.wait_ge(proj_done, count)
                if not (isinstance(r, int) and r <= 2):
                    act.wait_ge(sin_done, r - 2)
                H2 = P // 2
                act.copy(rot[0:H2, par, :], bank_in[H2:P, :])
                act.copy(rot[H2:P, par, :], bank_in[0:H2, :]).then_inc(rot_done, 1)

            def copy_v(u_next, j_next, bank_in, count):
                act.wait_ge(proj_done, count)
                act.copy(v_tok[:, j_next, :], bank_in[:, :]).then_inc(v_done, 1)

            def conv_copy(j, i, h, bank_in, count):
                act.wait_ge(proj_done, count)
                act.copy(y36[:, :, i % 2, h, :],
                         bank_in[:, 0:NB * NPAIR].rearrange("p (b n) -> p b n", b=NB)
                         ).then_inc(conv_done, 1)

            def exps(u, k):
                t = 4 * u + k
                act.wait_ge(max_done, t + 1)
                if not (isinstance(t, int) and t < 2):
                    act.wait_ge(pt_done, t - 1)
                for h in range(HG):
                    last = act.activation(prob[:, k % 2, h * P:(h + 1) * P],
                                          score_bank[k % 2][:, h * P:(h + 1) * P], ACT.Exp,
                                          bias=neg_max[:, k % 2, h:h + 1],
                                          accum_out=den[:, k % 2, h:h + 1])
                last.then_inc(exp_done, 1)

            for n, name in enumerate(ROPED):
                rotate(0, 0, name, proj_bank[n % 2], n + 1)
            conv_copy(0, 0, 0, proj_bank[5 % 2], 6)
            act.wait_ge(in_xt, 32)
            act.copy(x_hi[:, 1, :, :], x_raw[:, :, :]).then_inc(x_hi_done, 1)
            copy_v(0, 0, proj_bank[6 % 2], 7)
            split_wo(0)
            exps(0, 0)
            exps(0, 1)

            def unit(v, j, has_next, has_more):
                u = 2 * v + j
                items = BODY if has_next else LAST

                def item(name):
                    if name not in items:
                        return
                    at = items.index(name)
                    if name == "V":
                        copy_v(u + 1, 1 - j, item_bank(at), proj_count(u, at))
                    elif name == "C0":
                        conv_copy(1 - j, 0, 4 * v + 2 * j + 2, item_bank(at), proj_count(u, at))
                    elif name[0] == "C":
                        i = int(name[1])
                        conv_copy(j, i, 4 * v + 2 * j + i // 2, item_bank(at), proj_count(u, at))
                    else:
                        rotate(u + 1, j + 1, name, item_bank(at), proj_count(u, at))

                def head_copy(k):
                    t = 4 * u + k
                    act.wait_ge(pv_done, t + 1)
                    two_back(act, wo_done, u, k)
                    act.copy(head_hi[:, k % 2, :], headT_bank[:, :]).then_inc(head_hi_done, 1)

                item("K")
                item("Q0")
                head_copy(0)
                item("Q1")
                exps(u, 2)
                item("Q2")
                item("Q3")
                head_copy(1)
                item("C1")
                exps(u, 3)
                item("C2")
                if j == 0 and has_more:
                    split_w(v + 1, 0, proj_count(u, BODY.index("Q1")))
                item("C3")
                head_copy(2)
                if has_next:
                    exps(u + 1, 0)
                item("C0")
                if j == 1 and has_next:
                    split_wo(v + 1)
                item("V")
                head_copy(3)
                if j == 0 and has_more:
                    split_w(v + 1, 1, proj_count(u, BODY.index("V")))
                if has_next:
                    exps(u + 1, 1)

            phase_a(act, unit)

            def mix_query(b, j):
                act.wait_ge(x1T_done, b + 1)
                if not (isinstance(b, int) and b <= 1):
                    act.wait_ge(prod_done, b - 1)
                act.copy(qmix[:, j, :], mix_bank[:, 0:D]).then_inc(qmix_done, 1)

            def x2_copy(b, j):
                act.wait_ge(x2T_done, b + 1)
                act.copy(x2T[:, j, :], tf_bank[:, 0:D]).then_inc(x2copy_done, 1)

            def query_gate(b, j):
                act.wait_ge(qkvf_done, b + 1)
                if not (isinstance(b, int) and b == 0):
                    act.wait_ge(chosen_done, b)
                act.copy(gate[:, :], tf_bank[:, D:D + FH])
                act.mul(qf[:, j, :], tf_bank[:, 0:D], FD ** -0.5).then_inc(qf_done, 1)

            def gate_exp(b):
                act.wait_ge(gneg_done, b + 1)
                if not (isinstance(b, int) and b == 0):
                    act.wait_ge(gprob_done, b)
                act.activation(gexp[:, :], gate[:, :], ACT.Exp, bias=gneg[:, 0:1],
                               accum_out=gsum[:, 0:1]).then_inc(gexp_done, 1)

            def key_copy(b):
                act.wait_ge(ksT_done, b + 1)
                if not (isinstance(b, int) and b == 0):
                    act.wait_ge(kblock_done, b)
                act.copy(ksT[:, :], mix_bank[:, 0:P]).then_inc(kscopy_done, 1)

            def fexps(b, j, c):
                n = 4 * b + c
                act.wait_ge(fmax_done, n + 1)
                two_back_f(act, fpt_done, b, j, c)
                for h in range(4):
                    last = act.activation(prob[:, c % 2, h * P:(h + 1) * P],
                                          fscore_bank[c % 2][:, h * P:(h + 1) * P], ACT.Exp,
                                          bias=neg_max[:, c % 2, h:h + 1])
                last.then_inc(fexp_done, 1)

            def fprob_copy(b, j, c):
                n = 4 * b + c
                act.wait_ge(fpt_done, n + 1)
                two_back_f(act, y_done, b, j, c)
                act.copy(probT[:, c % 2, :], fprobT_bank[c % 2][:, :]).then_inc(fptcopy_done, 1)

            mix_query(0, 0)
            mix_query(1, 1)
            x2_copy(0, 0)
            query_gate(0, 0)
            gate_exp(0)
            key_copy(0)

            def seq(b, j, one, two):
                fexps(b, j, 0)
                if two:
                    mix_query(b + 2, j)
                fexps(b, j, 1)
                fprob_copy(b, j, 0)
                fexps(b, j, 2)
                if one:
                    x2_copy(b + 1, 1 - j)
                fprob_copy(b, j, 1)
                fexps(b, j, 3)
                if one:
                    query_gate(b + 1, 1 - j)
                fprob_copy(b, j, 2)
                if one:
                    gate_exp(b + 1)
                    key_copy(b + 1)
                fprob_copy(b, j, 3)

            phase_b(act, seq)

        @block.vector
        def _(dve):
            def take_cos(u_next, j_next, name, bank_in):
                r, par = rope_count(u_next, name), rope_parity(j_next, name)
                dve.wait_ge(rot_done, r)
                if not (isinstance(r, int) and r <= 2):
                    dve.wait_ge(rope_done, r - 2)
                dve.tensor_tensor(t_cos[:, par, :].rearrange("p (b t) -> p b t", b=BH),
                                  bank_in[:, :].rearrange("p (b t) -> p b t", b=BH),
                                  cos[:, :].unsqueeze(1).to_broadcast([P, BH, P]),
                                  ALU.mult).then_inc(cos_done, 1)

            def add_sin(u_next, j_next, name):
                r, par = rope_count(u_next, name), rope_parity(j_next, name)
                if name == "K":
                    dst = k_rope[:, j_next % 2, :]
                else:
                    dst = q_rope[:, j_next % 2, int(name[1]), :]
                dve.wait_ge(cos_done, r)
                dve.wait_ge(sin_done, r)
                dve.tensor_tensor(dst, t_cos[:, par, :], t_sin[:, par, :], ALU.add
                                  ).then_inc(rope_done, 1)

            dve.memset(half_pow[:, :], -0.5)
            dve.memset(vext[:, :, FD:FD + 1], 1.0).then_inc(const_set, 1)

            def split_lo(lo, raw, hi, hi_ready, count, done):
                dve.wait_ge(hi_ready, count)
                dve.tensor_tensor(lo, raw, hi.bitcast(FP32), ALU.subtract).then_inc(done, 1)

            def split_w(g, part):
                cols = slice(part * 3 * P, (part + 1) * 3 * P)
                split_lo(w_lo[:, :, cols], w_raw[:, :, cols], w_hi[:, :, cols], w_hi_done,
                         2 * g + part + 1, w_lo_done)

            def add_skip(u, j):
                dve.wait_ge(in_toep[j], 8 * (u - j) + 16)
                for hh in range(2):
                    last = dve.scalar_tensor_tensor(toep[:, j, hh, 0:P], anti[:, :],
                                                    dcoef[:, bass.ds(2 * u + hh, 1)],
                                                    toep[:, j, hh, 0:P], ALU.mult, ALU.add)
                last.then_inc(toep_done, 1)

            split_lo(x_lo[:, 0, :, :], x_raw[:, :, :], x_hi[:, 0, :, :], x_hi_done, 1, x_lo_done)
            split_w(0, 0)
            split_w(0, 1)
            dve.wait_ge(in_trig, 32)
            for n, name in enumerate(ROPED):
                take_cos(0, 0, name, proj_bank[n % 2])
                if n >= 1:
                    add_sin(0, 0, ROPED[n - 1])
            add_sin(0, 0, ROPED[-1])
            dve.wait_ge(in_skip, 32)
            add_skip(0, 0)

            def row_max(u, k):
                t = 4 * u + k
                dve.wait_ge(scores_done, t + 1)
                dve.tensor_reduce(neg_max[:, k % 2, :],
                                  score_bank[k % 2][:, :].rearrange("p (h k) -> p h k", h=HG),
                                  axis=AX.X, op=ALU.max, negate=True).then_inc(max_done, 1)

            def invert(u, k):
                t = 4 * u + k
                dve.wait_ge(exp_done, t + 1)
                dve.reciprocal(rden[:, k % 2, :], den[:, k % 2, :]).then_inc(rden_done, 1)

            row_max(0, 0)
            split_lo(x_lo[:, 1, :, :], x_raw[:, :, :], x_hi[:, 1, :, :], x_hi_done, 2, x_lo_done)
            row_max(0, 1)
            invert(0, 0)
            invert(0, 1)

            def unit(v, j, has_next, has_more):
                u = 2 * v + j

                def cos_item(name):
                    if has_next:
                        take_cos(u + 1, j + 1, name, item_bank(BODY.index(name)))

                def add_item(name):
                    if has_next:
                        add_sin(u + 1, j + 1, name)

                def prob_copy(k):
                    t = 4 * u + k
                    dve.wait_ge(pt_done, t + 1)
                    two_back(dve, pv_done, u, k)
                    dve.tensor_copy(probT[:, k % 2, :], probT_bank[:, :]).then_inc(ptcopy_done, 1)

                def head_low(k):
                    t = 4 * u + k
                    dve.wait_ge(head_hi_done, t + 1)
                    dve.tensor_tensor(head_lo[:, k % 2, :], headT_bank[:, :],
                                      head_hi[:, k % 2, :].bitcast(FP32), ALU.subtract
                                      ).then_inc(head_lo_done, 1)

                def accumulate(a):
                    dve.wait_ge(wo_done, 4 * u + 2 * a + 2)
                    if a == 0:
                        dve.wait_ge(in_x, 16)
                    own = x[:, j * BH + 2 * a:j * BH + 2 * a + 2, :]
                    dve.tensor_tensor(own, acc_bank[a][:, :].rearrange("p (b n) -> p b n", b=2), own,
                                      ALU.add).then_inc(acc_done, 1)

                prob_copy(0)
                cos_item("K")
                add_item("K")
                cos_item("Q0")
                head_low(0)
                add_item("Q0")
                row_max(u, 2)
                cos_item("Q1")
                add_item("Q1")
                invert(u, 2)
                prob_copy(1)
                if has_next:
                    add_skip(u + 1, 1 - j)
                cos_item("Q2")
                add_item("Q2")
                cos_item("Q3")
                head_low(1)
                add_item("Q3")
                row_max(u, 3)
                accumulate(0)
                invert(u, 3)
                prob_copy(2)
                if j == 0 and has_more:
                    split_w(v + 1, 0)
                head_low(2)
                if has_next:
                    row_max(u + 1, 0)
                prob_copy(3)
                if has_next:
                    invert(u + 1, 0)
                head_low(3)
                if j == 0 and has_more:
                    split_w(v + 1, 1)
                if has_next:
                    row_max(u + 1, 1)
                accumulate(1)
                if has_next:
                    invert(u + 1, 1)

            phase_a(dve, unit)

            dve.wait_ge(in_ffn, 64)
            dve.tensor_copy(causal[:, :], causal_raw[:, :])
            dve.tensor_copy(identb[:, :], ident[:, :]).then_inc(mask_done, 1)

            def norm_stats(s):
                if s == 1:
                    dve.wait_ge(ln1[3], 1)
                dve.wait_ge(acc_done, 2 * UNITS)
                for i in range(BH):
                    last = dve.bn_stats(stats[:, i, :], x[:, s * BH + i, :])
                last.then_inc(ln1[0], 1)
                dve.wait_ge(ln1[0], s + 1)
                for i in range(BH):
                    last = dve.bn_aggr(mean_var1[:, s * BH + i, :], stats[:, i, :])
                last.then_inc(ln1[1], 1)
                dve.wait_ge(ln1[1], s + 1)
                dve.tensor_scalar(var_eps[:, :], mean_var1[:, s * BH:(s + 1) * BH, 1], EPS, None, ALU.add
                                  ).then_inc(ln1[2], 1)

            def norm_first(b, j):
                if isinstance(b, int):
                    dve.wait_ge(ln1[3], b // BH + 1)
                else:
                    dve.wait_ge(ln1[3], NS)
                if not (isinstance(b, int) and b <= 1):
                    dve.wait_ge(x1T_done, b - 1)
                dve.tensor_scalar(x1[:, j, :], x[:, b, :], mean_var1[:, b, 0:1], rstd1[:, bass.ds(b, 1)],
                                  ALU.subtract, ALU.mult).then_inc(ln1[4], 1)

            def norm_one(ln, b, src, dst):
                dve.wait_ge(ln[0], b + 1)
                dve.bn_stats(stats[:, 0, :], src).then_inc(ln[1], 1)
                dve.wait_ge(ln[1], b + 1)
                dve.memset(carrier[:, :], 0.0)
                dve.bn_aggr(mean_var[:, :], stats[:, 0, :]).then_inc(ln[2], 1)
                dve.wait_ge(ln[2], b + 1)
                dve.tensor_scalar(var_eps[:, 0:1], mean_var[:, 1:2], EPS, None, ALU.add
                                  ).then_inc(ln[3], 1)
                dve.wait_ge(ln[4], b + 1)
                dve.tensor_scalar(dst, src, mean_var[:, 0:1], rstd[:, 0:1], ALU.subtract, ALU.mult
                                  ).then_inc(ln[5], 1)

            def mix_sum(b, j):
                dve.wait_ge(prod_done, b + 1)
                if not (isinstance(b, int) and b <= 1):
                    dve.wait_ge(mix_done, b - 1)
                dve.tensor_reduce(mixT[:, j, :], prod[:, j, :, :, :], axis=AX.X, op=ALU.add
                                  ).then_inc(mixT_done, 1)

            def mix_norm(b, j):
                dve.wait_ge(mix_done, b + 1)
                dve.wait_ge(ln1[4], b + 1)
                dve.tensor_tensor(x1[:, j, :], mix_bank[:, 0:D], x1[:, j, :], ALU.add).then_inc(ln2[0], 1)
                norm_one(ln2, b, x1[:, j, :], x2[:, j, :])

            def gating(b):
                dve.wait_ge(qf_done, b + 1)
                if not (isinstance(b, int) and b == 0):
                    dve.wait_ge(gexp_done, b)
                dve.tensor_reduce(gneg[:, 0:1], gate[:, :], axis=AX.X, op=ALU.max, negate=True
                                  ).then_inc(gneg_done, 1)
                dve.tensor_reduce(gtop[:, 0:1], gate[:, :], axis=AX.X, op=ALU.max).then_inc(gtop_done, 1)
                dve.wait_ge(gtop_done, b + 1)
                dve.scalar_tensor_tensor(gscore[:, :], gate[:, :], gtop[:, 0:1], ties[:, :],
                                         ALU.is_equal, ALU.mult).then_inc(gscore_done, 1)
                dve.wait_ge(gscore_done, b + 1)
                dve.tensor_reduce(gbest[:, 0:1], gscore[:, :], axis=AX.X, op=ALU.max
                                  ).then_inc(gbest_done, 1)
                dve.wait_ge(gbest_done, b + 1)
                dve.tensor_scalar(chosen[:, :], gscore[:, :], gbest[:, 0:1], None, ALU.is_equal
                                  ).then_inc(chosen_done, 1)
                dve.wait_ge(chosen_done, b + 1)

            def share(b, j):
                dve.tensor_tensor(kv_masked[:, :, :, :],
                                  kvf_bank[:, :].rearrange("p (n h d) -> p n h d", n=2, h=FH),
                                  chosen[:, :].unsqueeze(1).unsqueeze(3).to_broadcast([P, 2, FH, FD]),
                                  ALU.mult).then_inc(masked_done, 1)
                dve.wait_ge(masked_done, b + 1)
                dve.tensor_reduce(kv_shared[:, :, :],
                                  kv_masked[:, :, :, :].rearrange("p n h d -> p n d h"),
                                  axis=AX.X, op=ALU.add).then_inc(shared_done, 1)
                dve.wait_ge(shared_done, b + 1)
                if not (isinstance(b, int) and b == 0):
                    dve.wait_ge(ksT_done, b)
                dve.tensor_copy(krep[:, :, :], kv_shared[:, 0, :].unsqueeze(1).to_broadcast([P, FB, FD])
                                ).then_inc(krep_done, 1)
                dve.wait_ge(gexp_done, b + 1)
                dve.reciprocal(gprob[:, 0:1], gsum[:, 0:1]).then_inc(gprob_done, 1)
                dve.wait_ge(gprob_done, b + 1)
                dve.tensor_scalar(vext[:, j, 0:FD], kv_shared[:, 1, :], gprob[:, 0:1], None, ALU.mult
                                  ).then_inc(vext_done, 1)

            def frow_max(b, c):
                n = 4 * b + c
                dve.wait_ge(fscores_done, n + 1)
                dve.tensor_reduce(neg_max[:, c % 2, :],
                                  fscore_bank[c % 2][:, :].rearrange("p (h k) -> p h k", h=4),
                                  axis=AX.X, op=ALU.max, negate=True).then_inc(fmax_done, 1)

            def finish(b, j):
                dve.wait_ge(y_done, 4 * b + 4)
                y = y_bank[:, 0:FH * (FD + 1)].rearrange("p (h d) -> p h d", h=FH)
                dve.reciprocal(yden[:, :], y[:, :, FD]).then_inc(yden_done, 1)
                dve.wait_ge(yden_done, b + 1)
                dve.tensor_tensor(ynorm[:, :, :], y[:, :, 0:FD],
                                  yden[:, :].unsqueeze(2).to_broadcast([P, FH, FD]), ALU.mult
                                  ).then_inc(ynorm_done, 1)
                dve.wait_ge(ynorm_done, b + 1)
                dve.tensor_tensor(x2[:, j, :], ynorm[:, :, :].rearrange("p h d -> p (h d)"), x2[:, j, :],
                                  ALU.add).then_inc(ln3[0], 1)
                norm_one(ln3, b, x2[:, j, :], x[:, b, :])

            norm_stats(0)
            norm_first(0, 0)
            norm_first(1, 1)
            norm_stats(1)
            mix_sum(0, 0)
            mix_norm(0, 0)
            gating(0)
            share(0, 0)
            mix_sum(1, 1)

            def seq(b, j, one, two):
                if two:
                    norm_first(b + 2, j)
                frow_max(b, 0)
                frow_max(b, 1)
                if one:
                    mix_norm(b + 1, 1 - j)
                frow_max(b, 2)
                frow_max(b, 3)
                if one:
                    gating(b + 1)
                    share(b + 1, 1 - j)
                if two:
                    mix_sum(b + 2, j)
                finish(b, j)

            phase_b(dve, seq)

        @block.gpsimd
        def _(pool):
            def pairs(u_next, head, buf):
                if not (isinstance(u_next, int) and u_next <= 1):
                    pool.wait_ge(proj_done, proj_count(u_next - 2, BODY.index("C3")))
                src = ctxT[:, :, bass.ds(head * NB, 2 * NB), :]
                for d in range(HD):
                    at, n = PAIR_AT[d], HD - d
                    last = pool.tensor_tensor(kv[:, buf, :, :, at:at + n], src[:, :, :, 0:n],
                                              src[:, :, :, d:HD], ALU.mult)
                last.then_inc(kv_done, 1)

            def times_sin(u_next, j_next, name):
                r, par = rope_count(u_next, name), rope_parity(j_next, name)
                pool.wait_ge(rot_done, r)
                if not (isinstance(r, int) and r <= 2):
                    pool.wait_ge(rope_done, r - 2)
                pool.tensor_tensor(t_sin[:, par, :].rearrange("p (b t) -> p b t", b=BH),
                                   rot[:, par, :].rearrange("p (b t) -> p b t", b=BH),
                                   sin[:, :].unsqueeze(1).to_broadcast([P, BH, P]), ALU.mult
                                   ).then_inc(sin_done, 1)

            pool.wait_ge(in_ctx, 16)
            pairs(0, 0, 0)
            pool.wait_ge(in_trig, 32)
            for name in ROPED:
                times_sin(0, 0, name)

            def split_wo(g):
                pool.wait_ge(wo_hi_done, g + 1)
                heads = bass.ds(HG * g, HG)
                pool.tensor_tensor(wo_lo[:, heads, :], wo_raw[:, :, :], wo_hi[:, heads, :].bitcast(FP32),
                                   ALU.subtract).then_inc(wo_lo_done, 1)

            def normalize(u, k):
                pool.wait_ge(rden_done, 4 * u + k + 1)
                own = prob[:, k % 2, :].rearrange("p (h k) -> p h k", h=HG)
                pool.tensor_tensor(own, own, rden[:, k % 2, :].unsqueeze(2).to_broadcast([P, HG, P]),
                                   ALU.mult).then_inc(norm_done, 1)

            split_wo(0)
            normalize(0, 0)
            normalize(0, 1)

            def unit(v, j, has_next, has_more):
                u = 2 * v + j

                def sin_item(name):
                    if has_next:
                        times_sin(u + 1, j + 1, name)

                sin_item("K")
                sin_item("Q0")
                sin_item("Q1")
                normalize(u, 2)
                sin_item("Q2")
                sin_item("Q3")
                if has_next:
                    pairs(u + 1, 4 * v + 2 * j + 2, 1 - j)
                normalize(u, 3)
                if has_next:
                    normalize(u + 1, 0)
                if j == 1 and has_next:
                    split_wo(v + 1)
                if has_next:
                    normalize(u + 1, 1)

            phase_a(pool, unit)

            def power(dst, ready, done, count):
                width = dst.shape[1]
                pool.wait_ge(ready, count)
                pool.tensor_tensor(dst, var_eps[:, 0:width], half_pow[:, 0:width], ALU.pow
                                   ).then_inc(done, 1)

            def products(b, j):
                pool.wait_ge(qmix_done, b + 1)
                if not (isinstance(b, int) and b <= 1):
                    pool.wait_ge(mixT_done, b - 1)
                q = qmix[:, j, :].rearrange("p (a i) -> p a i", i=HD)
                pr = prod[:, j, :, :, :].rearrange("p a j i -> p a (j i)")
                y = y36[:, b, :, :, :].rearrange("p c h n -> p (c h) n")
                for d in range(HD):
                    at, n = PAIR_AT[d], HD - d
                    last = pool.tensor_tensor(pr[:, :, d * HD:d * HD + (n - 1) * (HD + 1) + 1:HD + 1],
                                              y[:, :, at:at + n], q[:, :, 0:n], ALU.mult)
                    if d:
                        last = pool.tensor_tensor(pr[:, :, d:d + (n - 1) * (HD + 1) + 1:HD + 1],
                                                  y[:, :, at:at + n], q[:, :, d:HD], ALU.mult)
                last.then_inc(prod_done, 1)

            def block_keys(b, j):
                pool.wait_ge(kscopy_done, b + 1)
                pool.tensor_tensor(kblock[:, j, :, :], ksT[:, :].unsqueeze(1).to_broadcast([P, FB, P]),
                                   blocks[:, :].unsqueeze(2).to_broadcast([P, FB, P]), ALU.mult
                                   ).then_inc(kblock_done, 1)

            pool.wait_ge(const_set, 1)
            power(rstd1[:, 0:BH], ln1[2], ln1[3], 1)
            power(rstd1[:, BH:NB], ln1[2], ln1[3], 2)
            pool.wait_ge(conv_done, CONV * UNITS)
            pool.wait_ge(scores_done, 4 * UNITS)
            products(0, 0)
            power(rstd[:, :], ln2[3], ln2[4], 1)
            products(1, 1)
            pool.wait_ge(in_ffn, 64)
            block_keys(0, 0)

            def seq(b, j, one, two):
                if one:
                    power(rstd[:, :], ln2[3], ln2[4], b + 2)
                if two:
                    products(b + 2, j)
                if one:
                    block_keys(b + 1, 1 - j)
                power(rstd[:, :], ln3[3], ln3[4], b + 1)

            phase_b(pool, seq)


def _layouts(a):
    import numpy as np
    f = np.float32
    x = np.asarray(a["x"]).reshape(NB * P, D)
    L = {}
    L["xt"] = x.T.reshape(C, P, NS, TOK).transpose(1, 2, 0, 3)
    L["x"] = x.reshape(NB, P, D).transpose(1, 0, 2)
    wq = np.asarray(a["L0_attn_Wq"]).reshape(NG, HG * P, D)
    wk = np.asarray(a["L0_attn_Wk"]).reshape(NG, P, D)
    wv = np.asarray(a["L0_attn_Wv"]).reshape(NG, P, D)
    w = np.concatenate([wk, wq, wv], axis=1)
    L["wqkv"] = w.transpose(0, 2, 1).reshape(NG, C, P, 6 * P).transpose(2, 0, 1, 3)
    L["wo"] = np.asarray(a["L0_attn_Wo"]).T.reshape(NH, P, D).transpose(1, 0, 2)
    filt = np.asarray(a["L0_xattn_ssm_kernel"])
    padded = np.concatenate([np.zeros((XH, P - 1), f), filt], axis=1)
    L["toep"] = np.stack([padded[:, p:p + D] for p in range(P)])
    L["dcoef"] = np.broadcast_to(np.asarray(a["L0_xattn_D"])[None, :], (P, XH))
    c = np.asarray(a["ctx_2048"]).reshape(NB, XH, HD, C, P)[..., ::-1]
    L["ctx"] = c.transpose(4, 3, 1, 0, 2).reshape(P, C, XH * NB, HD)
    wf = np.concatenate([np.asarray(a["L0_ffn_W_qkv"]), np.asarray(a["L0_ffn_W_gate"])], axis=0)
    L["wf"] = wf.T.reshape(C, P, 3 * D + FH).transpose(1, 0, 2)
    inv = (f(1.0) / f(10000.0) ** (np.arange(0, P, 2, dtype=f) / f(P))).astype(f)
    angle = np.repeat(np.arange(P, dtype=f)[:, None] * inv[None, :], 2, axis=1).T
    root = float(P) ** -0.25
    sign = np.where(np.arange(P) < P // 2, -1.0, 1.0)[:, None]
    L["cos"] = (np.cos(angle).astype(np.float64) * root).astype(f)
    L["sin"] = (np.sin(angle).astype(np.float64) * root * sign).astype(f)
    L["ident"] = np.eye(P, dtype=f)
    L["anti"] = np.eye(P, dtype=f)[::-1]
    L["causal"] = np.where(np.tril(np.ones((P, P))) > 0, 0.0, -1e30).astype(f)
    L["blocks"] = (np.arange(P)[:, None] // FD == np.arange(FB)[None, :]).astype(f)
    L["ties"] = np.broadcast_to(np.arange(FH, 0, -1).astype(f)[None, :], (P, FH))
    return {k: np.ascontiguousarray(v) for k, v in L.items()}


def kernel(**inputs):
    import concourse.bacc as bacc
    from concourse.bass_utils import run_bass_kernel_spmd
    nc = bacc.Bacc("TRN2", target_bir_lowering=False, num_devices=1)
    arrays, args = {}, []
    for name, a in _layouts(inputs).items():
        arrays[f"in_{name}"] = a
        args.append(nc.dram_tensor(f"in_{name}", a.shape, mybir.dt.from_np(a.dtype),
                                   kind="ExternalInput").ap())
    out = nc.dram_tensor("out", (NB, P, D), FP32, kind="ExternalOutput").ap()
    decoder_kernel(nc, *args, out)
    result = run_bass_kernel_spmd(nc, [arrays], core_ids=[0])
    return result.results[0]["out"]
```

```python
import concourse.bass as bass
from concourse import mybir
from contextlib import ExitStack

FP32 = mybir.dt.float32
BF16 = mybir.dt.bfloat16
FP32R = mybir.dt.float32r
ALU = mybir.AluOpType
ACT = mybir.ActivationFunctionType
AX = mybir.AxisListType

P = 128
NB = 8
D = 256
C = D // P
NG = 4
HG = 4
NH = NG * HG
NS = 2
BH = NB // NS
TOK = BH * P
UNITS = NG * NS
XH = 16
HD = 8
NPAIR = HD * (HD + 1) // 2
PAIR_AT = [sum(HD - e for e in range(d)) for d in range(HD)]
FH = 16
FD = 16
FB = P // FD
FC = 4
CW = FC * FD
EPS = 1e-5
CONV = 4

COLS = ["K", "Q0", "Q1", "Q2", "Q3", "V"]
FRONT = ["K", "Q0", "Q1", "Q2", "Q3", "C0", "V"]
BODY = ["K", "Q0", "Q1", "Q2", "Q3", "C1", "C2", "C3", "C0", "V"]
LAST = ["C1", "C2", "C3"]
ROPED = ["K", "Q0", "Q1", "Q2", "Q3"]


def decoder_kernel(nc, xt_d, x_d, wqkv_d, wo_d, toep_d, dcoef_d, ctx_d, wf_d, cos_d, sin_d, ident_d,
                   anti_d, causal_d, blocks_d, ties_d, out_d):
    ctx = ExitStack()
    with ctx:
        def sb(name, shape, dt=FP32):
            return ctx.enter_context(nc.sbuf_tensor(name, shape, dt))

        def sem(name):
            return ctx.enter_context(nc.semaphore(name))

        x_raw = sb("x_raw", [P, C, TOK])
        x_hi = sb("x_hi", [P, NS, C, TOK], FP32R)
        x_lo = sb("x_lo", [P, NS, C, TOK], FP32R)
        x = sb("x", [P, NB, D])
        w_raw = sb("w_raw", [P, C, 6 * P])
        w_hi = sb("w_hi", [P, C, 6 * P], FP32R)
        w_lo = sb("w_lo", [P, C, 6 * P], FP32R)
        wo_raw = sb("wo_raw", [P, HG, D])
        wo_hi = sb("wo_hi", [P, NH, D], FP32R)
        wo_lo = sb("wo_lo", [P, NH, D], FP32R)
        toep = sb("toep", [P, 2, 2, D])
        dcoef = sb("dcoef", [P, XH])
        ctxT = sb("ctxT", [P, C, XH * NB, HD])
        kv = sb("kv", [P, 2, C, 2 * NB, NPAIR])
        y36 = sb("y36", [P, NB, C, XH, NPAIR])
        cos = sb("cos", [P, P])
        sin = sb("sin", [P, P])
        ident = sb("ident", [P, P])
        anti = sb("anti", [P, P])
        identb = sb("identb", [P, P], BF16)
        causal_raw = sb("causal_raw", [P, P])
        causal = sb("causal", [P, P], BF16)
        blocks = sb("blocks", [P, FC])
        ties = sb("ties", [P, FH])
        q_rope = sb("q_rope", [P, 2, HG, TOK])
        k_rope = sb("k_rope", [P, 2, TOK])
        v_tok = sb("v_tok", [P, 2, TOK])
        rot = sb("rot", [P, 2, TOK])
        t_cos = sb("t_cos", [P, 2, TOK])
        t_sin = sb("t_sin", [P, 2, TOK])
        neg_max = sb("neg_max", [P, 2, HG])
        den = sb("den", [P, 2, HG])
        rden = sb("rden", [P, 2, HG])
        prob = sb("prob", [P, 2, HG * P])
        probT = sb("probT", [P, 2, HG * P])
        head_hi = sb("head_hi", [P, 2, HG * P], FP32R)
        head_lo = sb("head_lo", [P, 2, HG * P], FP32R)
        stats = sb("stats", [P, BH, 6])
        mean_var1 = sb("mean_var1", [P, NB, 2])
        rstd1 = sb("rstd1", [P, NB])
        stats_of = [sb(f"stats{n}", [P, 6]) for n in (2, 3)]
        mean_var_of = [sb(f"mean_var{n}", [P, 2]) for n in (2, 3)]
        var_eps1 = sb("var_eps1", [P, NB])
        var_eps_of = [sb(f"var_eps{n}", [P, 1]) for n in (2, 3)]
        rstd_of = [sb(f"rstd{n}", [P, 1]) for n in (2, 3)]
        half_pow = sb("half_pow", [P, BH])
        carrier = sb("carrier", [P, 1])
        prod = q_rope[:, :, :, :].rearrange("p n h t -> p n (h t)").rearrange(
            "p n (a j i) -> p n a j i", j=HD, i=HD)
        kblock = x_hi[:, :, :, :].rearrange("p j n (h k) -> p j n h k", k=P)
        wf = sb("wf", [P, C, 3 * D + FH])
        qmix = rot[:, :, 0:D]
        mixT = t_cos[:, :, 0:D]
        x1 = v_tok[:, :, 0:D]
        x2 = v_tok[:, :, D:2 * D]
        x2T = k_rope[:, :, 0:D]
        qf = w_hi[:, :, 0:FC * P].rearrange("p j (c t) -> p j c t", t=P)
        gate = sb("gate", [P, FH])
        gexp = sb("gexp", [P, FH])
        gtop = sb("gtop", [P, 1])
        gneg = sb("gneg", [P, 1])
        gsum = sb("gsum", [P, 1])
        gprob = sb("gprob", [P, 1])
        gscore = sb("gscore", [P, FH])
        gbest = sb("gbest", [P, 1])
        chosen = sb("chosen", [P, FH])
        kv_masked = sb("kv_masked", [P, 2, FH, FD])
        kv_shared = sb("kv_shared", [P, 2, FD])
        krep = sb("krep", [P, FB, FD])
        ksT = sb("ksT", [P, P])
        ksT_hi = sb("ksT_hi", [P, P], FP32R)
        ksT_lo = sb("ksT_lo", [P, P], FP32R)
        vext = sb("vext", [P, NB, FD + 1])
        yden = sb("yden", [P, FH])
        ynorm = sb("ynorm", [P, FH, FD])

        bank = [ctx.enter_context(nc.psum_tensor(f"bank{i}", [P, 512], FP32)) for i in range(8)]
        proj_bank = [bank[0], bank[1]]
        score_bank = [bank[2], bank[3]]
        probT_bank, headT_bank = bank[4], bank[5]
        acc_bank = [bank[6], bank[7]]
        fscore_bank = [bank[4], bank[5]]
        fprobT_bank = [bank[2], bank[3]]
        mix_bank, tf_bank, kvf_bank, y_bank = bank[0], bank[1], bank[6], bank[7]

        in_xt = sem("in_xt")
        x_hi_done = sem("x_hi_done")
        x_lo_done = sem("x_lo_done")
        w_hi_done = sem("w_hi_done")
        w_lo_done = sem("w_lo_done")
        wo_hi_done = sem("wo_hi_done")
        wo_lo_done = sem("wo_lo_done")
        in_w = sem("in_w")
        in_wo = sem("in_wo")
        in_trig = sem("in_trig")
        in_ident = sem("in_ident")
        in_toep = [sem("in_toep0"), sem("in_toep1")]
        in_skip = sem("in_skip")
        in_ctx = sem("in_ctx")
        in_x = sem("in_x")
        in_ffn = sem("in_ffn")
        mask_done = sem("mask_done")
        const_set = sem("const_set")
        toep_done = sem("toep_done")
        proj_done = sem("proj_done")
        rot_done = sem("rot_done")
        cos_done = sem("cos_done")
        sin_done = sem("sin_done")
        rope_done = sem("rope_done")
        v_done = sem("v_done")
        conv_done = sem("conv_done")
        kv_done = sem("kv_done")
        scores_done = sem("scores_done")
        max_done = sem("max_done")
        exp_done = sem("exp_done")
        rden_done = sem("rden_done")
        norm_done = sem("norm_done")
        pt_done = sem("pt_done")
        ptcopy_done = sem("ptcopy_done")
        pv_done = sem("pv_done")
        head_hi_done = sem("head_hi_done")
        head_lo_done = sem("head_lo_done")
        wo_done = sem("wo_done")
        acc_done = sem("acc_done")
        ln1 = [sem(f"ln1_{n}") for n in ("stats", "aggr", "eps", "rstd", "out")]
        ln2 = [sem(f"ln2_{n}") for n in ("sum", "stats", "aggr", "eps", "rstd", "out")]
        ln3 = [sem(f"ln3_{n}") for n in ("sum", "stats", "aggr", "eps", "rstd", "out")]
        x1T_done = sem("x1T_done")
        qmix_done = sem("qmix_done")
        prod_done = sem("prod_done")
        mixT_done = sem("mixT_done")
        mix_done = sem("mix_done")
        x2T_done = sem("x2T_done")
        x2_kept = sem("x2_kept")
        x2copy_done = sem("x2copy_done")
        gate_mm_done = sem("gate_mm_done")
        gate_done = sem("gate_done")
        kvf_done = sem("kvf_done")
        qT_done = sem("qT_done")
        qf_hi_done = sem("qf_hi_done")
        qf_lo_done = sem("qf_lo_done")
        gtop_done = sem("gtop_done")
        gneg_done = sem("gneg_done")
        gexp_done = sem("gexp_done")
        gprob_done = sem("gprob_done")
        gscore_done = sem("gscore_done")
        gbest_done = sem("gbest_done")
        chosen_done = sem("chosen_done")
        masked_done = sem("masked_done")
        shared_done = sem("shared_done")
        krep_done = sem("krep_done")
        vext_done = sem("vext_done")
        ksT_done = sem("ksT_done")
        kscopy_done = sem("kscopy_done")
        ks_lo_done = sem("ks_lo_done")
        kblock_done = sem("kblock_done")
        fscores_done = sem("fscores_done")
        fmax_done = sem("fmax_done")
        fexp_done = sem("fexp_done")
        fpt_done = sem("fpt_done")
        fptcopy_done = sem("fptcopy_done")
        y_done = sem("y_done")
        yden_done = sem("yden_done")
        ynorm_done = sem("ynorm_done")
        stored = sem("stored")

        def proj_count(u, i):
            return len(FRONT) + len(BODY) * u + i + 1

        def item_bank(i):
            return proj_bank[(len(FRONT) + i) % 2]

        def rope_count(u_next, name):
            return len(ROPED) * u_next + ROPED.index(name) + 1

        def rope_parity(j_next, name):
            return (len(ROPED) * j_next + ROPED.index(name)) % 2

        def two_back(eng, done, n, k):
            if k >= 2:
                eng.wait_ge(done, 4 * n + k - 1)

        def at_least(eng, done, n, back):
            if not (isinstance(n, int) and n < back):
                eng.wait_ge(done, n - back + 1)

        def has(b, ahead):
            return not isinstance(b, int) or b + ahead < NB

        block = ctx.enter_context(nc.Block())

        def phase_a(eng, unit):
            with eng.Fori(0, NG - 1, 1) as v:
                unit(v, 0, True, True)
                unit(v, 1, True, True)
            unit(NG - 1, 0, True, False)
            unit(NG - 1, 1, False, False)

        def phase_b(eng, seq):
            with eng.Fori(0, NB // 2 - 2, 1) as w:
                seq(2 * w, 0)
                seq(2 * w + 1, 1)
            for b in range(NB - 4, NB):
                seq(b, b % 2)

        @block.sync
        def _(sp):
            def load_toep(u, j):
                if not (isinstance(u, int) and u <= 1):
                    sp.wait_ge(proj_done, proj_count(u - 2, BODY.index("C3")))
                sp.dma_start(toep[:, j, :, :], toep_d[:, bass.ds(2 * u, 2), :]).then_inc(in_toep[j], 16)

            sp.dma_start(x_raw[:, :, :], xt_d[:, 0, :, :]).then_inc(in_xt, 16)
            sp.dma_start(cos[:, :], cos_d).then_inc(in_trig, 16)
            sp.dma_start(sin[:, :], sin_d).then_inc(in_trig, 16)
            sp.dma_start(ctxT[:, :, :, :], ctx_d).then_inc(in_ctx, 16)
            load_toep(0, 0)
            sp.dma_start(dcoef[:, :], dcoef_d).then_inc(in_skip, 16)
            sp.dma_start(anti[:, :], anti_d).then_inc(in_skip, 16)
            sp.dma_start(ident[:, :], ident_d).then_inc(in_ident, 16)
            sp.wait_ge(x_lo_done, 1)
            sp.dma_start(x_raw[:, :, :], xt_d[:, 1, :, :]).then_inc(in_xt, 16)
            sp.dma_start(wo_raw[:, :, :], wo_d[:, 0:HG, :]).then_inc(in_wo, 16)
            load_toep(1, 1)
            sp.dma_start(x[:, :, :], x_d).then_inc(in_x, 16)
            with sp.Fori(0, NG - 1, 1) as v:
                sp.wait_ge(w_lo_done, 2 * v + 2)
                sp.dma_start(w_raw[:, :, :], wqkv_d[:, v + 1, :, :]).then_inc(in_w, 16)
                sp.wait_ge(wo_lo_done, v + 1)
                sp.dma_start(wo_raw[:, :, :], wo_d[:, bass.ds(HG * v + HG, HG), :]).then_inc(in_wo, 16)
                load_toep(2 * v + 2, 0)
                load_toep(2 * v + 3, 1)
            sp.dma_start(wf[:, :, :], wf_d).then_inc(in_ffn, 16)
            sp.dma_start(causal_raw[:, :], causal_d).then_inc(in_ffn, 16)
            sp.dma_start(blocks[:, :], blocks_d).then_inc(in_ffn, 16)
            sp.dma_start(ties[:, :], ties_d).then_inc(in_ffn, 16)

            with sp.Fori(0, NB, 1) as b:
                sp.wait_ge(ln3[5], b + 1)
                sp.dma_start(out_d[b, :, :], x[:, b, :]).then_inc(stored, 16)
            sp.wait_ge(stored, 16 * NB)

        @block.tensor
        def _(pe):
            def project(j, name, out):
                col = COLS.index(name) * P
                if name == "V":
                    for b in range(BH):
                        tok = slice(b * P, (b + 1) * P)
                        for c in range(C):
                            for n, (xp, wp) in enumerate(((x_hi, w_hi), (x_hi, w_lo), (x_lo, w_hi))):
                                last = pe.matmul(out[:, tok], xp[:, j, c, tok], wp[:, c, col:col + P],
                                                 start=(c + n == 0), stop=(c == C - 1 and n == 2))
                else:
                    for c in range(C):
                        for n, (wp, xp) in enumerate(((w_hi, x_hi), (w_hi, x_lo), (w_lo, x_hi))):
                            last = pe.matmul(out[:, :], wp[:, c, col:col + P], xp[:, j, c, :],
                                             start=(c + n == 0), stop=(c == C - 1 and n == 2))
                last.then_inc(proj_done, 1)

            def conv(j, i, bank_out):
                hh, lb = i // 2, i % 2
                out = bank_out[:, 0:NB * NPAIR]
                for m in range(lb + 1):
                    tap = (lb - m) * P
                    last = pe.matmul(out, toep[:, j, hh, tap:tap + P],
                                     kv[:, j, m, hh * NB:(hh + 1) * NB, :],
                                     start=(m == 0), stop=(m == lb))
                last.then_inc(proj_done, 1)

            def scores(u, j, k):
                if k == 0:
                    pe.wait_ge(rope_done, len(ROPED) * (u + 1))
                if isinstance(u, int) and 4 * u + k < 2:
                    pass
                else:
                    pe.wait_ge(exp_done, 4 * u + k - 1)
                for h in range(HG):
                    last = pe.matmul(score_bank[k % 2][:, h * P:(h + 1) * P],
                                     q_rope[:, j, h, k * P:(k + 1) * P],
                                     k_rope[:, j, k * P:(k + 1) * P], start=True, stop=True)
                last.then_inc(scores_done, 1)

            pe.wait_ge(x_lo_done, 1)
            for n, name in enumerate(FRONT):
                if n >= 2:
                    pe.wait_ge(cos_done, n - 1)
                if name in ("K", "Q2"):
                    pe.wait_ge(w_lo_done, 1 if name == "K" else 2)
                if name == "C0":
                    pe.wait_ge(kv_done, 1)
                    pe.wait_ge(toep_done, 1)
                    conv(0, 0, proj_bank[n % 2])
                else:
                    project(0, name, proj_bank[n % 2])
            scores(0, 0, 0)
            scores(0, 0, 1)

            def bank_free(u, items, i):
                if i >= 2:
                    name, un = items[i - 2], u + 1
                else:
                    name, un = BODY[len(BODY) - 2 + i], u
                if name == "V":
                    pe.wait_ge(v_done, un + 1)
                elif name == "C0":
                    pe.wait_ge(conv_done, CONV * un + 1)
                elif name[0] == "C":
                    pe.wait_ge(conv_done, CONV * u + int(name[1]) + 1)
                else:
                    pe.wait_ge(cos_done, rope_count(un, name))

            def unit(v, j, has_next, has_more):
                u = 2 * v + j
                items = BODY if has_next else LAST

                def item(name):
                    if name not in items:
                        return
                    i = items.index(name)
                    bank_free(u, items, i)
                    if name == "C0":
                        pe.wait_ge(kv_done, u + 2)
                        pe.wait_ge(toep_done, u + 2)
                        conv(1 - j, 0, item_bank(i))
                    elif name[0] == "C":
                        conv(j, int(name[1]), item_bank(i))
                    else:
                        if name == "K" and j == 0:
                            pe.wait_ge(x_lo_done, 2)
                        if name in ("K", "Q2") and j == 1:
                            pe.wait_ge(w_lo_done, 2 * v + (3 if name == "K" else 4))
                        project(1 - j, name, item_bank(i))

                def turn(k):
                    t = 4 * u + k
                    pe.wait_ge(norm_done, t + 1)
                    if k:
                        pe.wait_ge(ptcopy_done, t)
                    for h in range(HG):
                        last = pe.transpose(probT_bank[:, h * P:(h + 1) * P],
                                            prob[:, k % 2, h * P:(h + 1) * P], ident[:, :])
                    last.then_inc(pt_done, 1)

                def values(k):
                    t = 4 * u + k
                    if k == 0:
                        pe.wait_ge(v_done, u + 1)
                    pe.wait_ge(ptcopy_done, t + 1)
                    if k:
                        pe.wait_ge(head_lo_done, t)
                    pe.matmul(headT_bank[:, :], v_tok[:, j, k * P:(k + 1) * P], probT[:, k % 2, :],
                              start=True, stop=True).then_inc(pv_done, 1)

                def output(k):
                    t = 4 * u + k
                    if k == 0:
                        pe.wait_ge(wo_lo_done, v + 1)
                    pe.wait_ge(head_lo_done, t + 1)
                    for h in range(HG):
                        for n, (hp, wp) in enumerate(((head_hi, wo_hi), (head_hi, wo_lo),
                                                      (head_lo, wo_hi))):
                            last = pe.matmul(acc_bank[k // 2][:, (k % 2) * D:(k % 2 + 1) * D],
                                             hp[:, k % 2, h * P:(h + 1) * P], wp[:, 4 * v + h, :],
                                             start=(h + n == 0), stop=(h == HG - 1 and n == 2))
                    last.then_inc(wo_done, 1)

                if not has_next:
                    item("C1")
                    turn(0)
                    item("C2")
                    item("C3")
                    values(0)
                    scores(u, j, 2)
                    pe.wait_ge(conv_done, CONV * UNITS)
                    x1_turn(0, 0)
                    turn(1)
                    scores(u, j, 3)
                    output(0)
                    values(1)
                    x1_turn(1, 1)
                    output(1)
                    turn(2)
                    values(2)
                    turn(3)
                    output(2)
                    values(3)
                    output(3)
                    mix_turn(0, 0)
                    return

                item("K")
                turn(0)
                item("Q0")
                values(0)
                item("Q1")
                scores(u, j, 2)
                output(0)
                item("Q2")
                turn(1)
                item("Q3")
                values(1)
                item("C1")
                scores(u, j, 3)
                output(1)
                item("C2")
                turn(2)
                item("C3")
                values(2)
                if has_next:
                    scores(u + 1, 1 - j, 0)
                item("C0")
                turn(3)
                output(2)
                values(3)
                item("V")
                if has_next:
                    scores(u + 1, 1 - j, 1)
                output(3)

            pe.wait_ge(in_ident, 16)


            def x1_turn(b, j):
                pe.wait_ge(ln1[4], b + 1)
                if isinstance(b, int) and b == 1:
                    pe.wait_ge(qmix_done, 1)
                else:
                    at_least(pe, x2copy_done, b, 2)
                for c in range(C):
                    last = pe.transpose(mix_bank[:, c * P:(c + 1) * P], x1[:, j, c * P:(c + 1) * P],
                                        ident[:, :])
                last.then_inc(x1T_done, 1)

            def mix_turn(b, j):
                pe.wait_ge(mixT_done, b + 1)
                pe.wait_ge(qmix_done, NB if isinstance(b, int) and b == NB - 1 else b + 2)
                for c in range(C):
                    last = pe.transpose(mix_bank[:, c * P:(c + 1) * P], mixT[:, j, c * P:(c + 1) * P],
                                        ident[:, :])
                last.then_inc(mix_done, 1)

            def x2_turn(b, j):
                pe.wait_ge(ln2[5], b + 1)
                for c in range(C):
                    last = pe.transpose(mix_bank[:, c * P:(c + 1) * P], x2[:, j, c * P:(c + 1) * P],
                                        ident[:, :])
                last.then_inc(x2T_done, 1)

            def gate_project(b, j):
                pe.wait_ge(x2copy_done, b + 1)
                at_least(pe, qf_lo_done, b, 1)
                for c in range(C):
                    last = pe.matmul(tf_bank[:, D:D + FH], x2T[:, j, c * P:(c + 1) * P],
                                     wf[:, c, 3 * D:3 * D + FH], start=(c == 0), stop=(c == C - 1))
                last.then_inc(gate_mm_done, 1)

            def kv_project(b, j, c):
                if c == 0:
                    at_least(pe, masked_done, b, 1)
                last = pe.matmul(kvf_bank[:, :], x2T[:, j, c * P:(c + 1) * P], wf[:, c, D:3 * D],
                                 start=(c == 0), stop=(c == C - 1))
                if c == C - 1:
                    last.then_inc(kvf_done, 1)

            def query_project(b, j):
                pe.wait_ge(kscopy_done, b + 1)
                for n in range(C):
                    for c in range(C):
                        last = pe.matmul(tf_bank[:, n * P:(n + 1) * P], wf[:, c, n * P:(n + 1) * P],
                                         x2T[:, j, c * P:(c + 1) * P], start=(c == 0), stop=(c == C - 1))
                last.then_inc(qT_done, 1)

            def key_turn(b):
                pe.wait_ge(krep_done, b + 1)
                pe.transpose(tf_bank[:, 0:P], krep[:, :, :].rearrange("p n d -> p (n d)"),
                             ident[:, :]).then_inc(ksT_done, 1)

            def fscores(b, j, c):
                if c == 0:
                    pe.wait_ge(kblock_done, b + 1)
                    pe.wait_ge(qf_lo_done, b + 1)
                out = fscore_bank[c % 2]
                own = slice(CW * (c % 2), CW * (c % 2 + 1))
                pe.matmul(out[:, :], qf[:, j, c, :], kblock[:, j, 0, :, :], start=True, stop=False)
                pe.matmul(out[:, :], qf[own, j, c, :], kblock[own, j, 1, :, :], start=False, stop=False)
                pe.matmul(out[:, :].rearrange("p (h k) -> p h k", k=P), identb[:, :],
                          causal[:, :].unsqueeze(1).to_broadcast([P, 4, P]),
                          start=False, stop=True).then_inc(fscores_done, 1)

            def fturn(b, c):
                pe.wait_ge(fexp_done, 4 * b + c + 1)
                for h in range(4):
                    last = pe.transpose(fprobT_bank[c % 2][:, h * P:(h + 1) * P],
                                        prob[:, c % 2, h * P:(h + 1) * P], ident[:, :])
                last.then_inc(fpt_done, 1)

            def fvalues(b, c):
                pe.wait_ge(fptcopy_done, 4 * b + c + 1)
                if c == 0:
                    pe.wait_ge(vext_done, b + 1)
                    at_least(pe, ynorm_done, b, 1)
                for h in range(4):
                    f = 4 * c + h
                    last = pe.matmul(y_bank[:, f * (FD + 1):(f + 1) * (FD + 1)],
                                     probT[:, c % 2, h * P:(h + 1) * P], vext[:, b, :],
                                     start=True, stop=True)
                last.then_inc(y_done, 1)

            phase_a(pe, unit)

            pe.wait_ge(in_ffn, 64)
            x2_turn(0, 0)
            gate_project(0, 0)
            x1_turn(2, 0)
            pe.wait_ge(acc_done, 2 * UNITS)
            kv_project(0, 0, 0)
            kv_project(0, 0, 1)
            mix_turn(1, 1)
            key_turn(0)
            query_project(0, 0)
            x2_turn(1, 1)
            x1_turn(3, 1)
            gate_project(1, 1)
            pe.wait_ge(mask_done, 1)
            fscores(0, 0, 0)
            fscores(0, 0, 1)
            kv_project(1, 1, 0)
            kv_project(1, 1, 1)
            fturn(0, 0)
            mix_turn(2, 0)
            fscores(0, 0, 2)
            key_turn(1)

            def seq(b, j):
                if has(b, 1):
                    query_project(b + 1, 1 - j)
                fturn(b, 1)
                fscores(b, j, 3)
                if has(b, 2):
                    x2_turn(b + 2, j)
                fvalues(b, 0)

                fvalues(b, 1)
                if has(b, 4):
                    x1_turn(b + 4, j)
                fturn(b, 2)
                if has(b, 1):
                    fscores(b + 1, 1 - j, 0)
                if has(b, 2):
                    gate_project(b + 2, j)
                    kv_project(b + 2, j, 0)
                    kv_project(b + 2, j, 1)

                fvalues(b, 2)
                fturn(b, 3)
                if has(b, 1):
                    fscores(b + 1, 1 - j, 1)
                if has(b, 3):
                    mix_turn(b + 3, 1 - j)

                fvalues(b, 3)
                if has(b, 1):
                    fturn(b + 1, 0)
                if has(b, 2):
                    key_turn(b + 2)
                if has(b, 1):
                    fscores(b + 1, 1 - j, 2)

            phase_b(pe, seq)

        @block.scalar
        def _(act):
            act.dma_start(w_raw[:, :, :], wqkv_d[:, 0, :, :]).then_inc(in_w, 16)

            def split_w(g, part, uses):
                if part == 0:
                    act.wait_ge(in_w, 16 * g + 16)
                if uses is not None:
                    act.wait_ge(proj_done, uses)
                cols = slice(part * 3 * P, (part + 1) * 3 * P)
                act.copy(w_hi[:, :, cols], w_raw[:, :, cols]).then_inc(w_hi_done, 1)

            def split_wo(g):
                act.wait_ge(in_wo, 16 * g + 16)
                act.copy(wo_hi[:, bass.ds(HG * g, HG), :], wo_raw[:, :, :]).then_inc(wo_hi_done, 1)

            act.wait_ge(in_xt, 16)
            act.copy(x_hi[:, 0, :, :], x_raw[:, :, :]).then_inc(x_hi_done, 1)
            split_w(0, 0, None)
            split_w(0, 1, None)

            def rotate(u_next, j_next, name, bank_in, count):
                r, par = rope_count(u_next, name), rope_parity(j_next, name)
                act.wait_ge(proj_done, count)
                if not (isinstance(r, int) and r <= 2):
                    act.wait_ge(sin_done, r - 2)
                H2 = P // 2
                act.copy(rot[0:H2, par, :], bank_in[H2:P, :])
                act.copy(rot[H2:P, par, :], bank_in[0:H2, :]).then_inc(rot_done, 1)

            def copy_v(u_next, j_next, bank_in, count):
                act.wait_ge(proj_done, count)
                act.copy(v_tok[:, j_next, :], bank_in[:, :]).then_inc(v_done, 1)

            def conv_copy(j, i, h, bank_in, count):
                act.wait_ge(proj_done, count)
                act.copy(y36[:, :, i % 2, h, :],
                         bank_in[:, 0:NB * NPAIR].rearrange("p (b n) -> p b n", b=NB)
                         ).then_inc(conv_done, 1)

            def exps(u, k):
                t = 4 * u + k
                act.wait_ge(max_done, t + 1)
                if not (isinstance(t, int) and t < 2):
                    act.wait_ge(pt_done, t - 1)
                for h in range(HG):
                    last = act.activation(prob[:, k % 2, h * P:(h + 1) * P],
                                          score_bank[k % 2][:, h * P:(h + 1) * P], ACT.Exp,
                                          bias=neg_max[:, k % 2, h:h + 1],
                                          accum_out=den[:, k % 2, h:h + 1])
                last.then_inc(exp_done, 1)

            for n, name in enumerate(ROPED):
                rotate(0, 0, name, proj_bank[n % 2], n + 1)
            conv_copy(0, 0, 0, proj_bank[5 % 2], 6)
            act.wait_ge(in_xt, 32)
            act.copy(x_hi[:, 1, :, :], x_raw[:, :, :]).then_inc(x_hi_done, 1)
            copy_v(0, 0, proj_bank[6 % 2], 7)
            split_wo(0)
            exps(0, 0)
            exps(0, 1)

            def unit(v, j, has_next, has_more):
                u = 2 * v + j
                items = BODY if has_next else LAST

                def item(name):
                    if name not in items:
                        return
                    at = items.index(name)
                    if name == "V":
                        copy_v(u + 1, 1 - j, item_bank(at), proj_count(u, at))
                    elif name == "C0":
                        conv_copy(1 - j, 0, 4 * v + 2 * j + 2, item_bank(at), proj_count(u, at))
                    elif name[0] == "C":
                        i = int(name[1])
                        conv_copy(j, i, 4 * v + 2 * j + i // 2, item_bank(at), proj_count(u, at))
                    else:
                        rotate(u + 1, j + 1, name, item_bank(at), proj_count(u, at))

                def head_copy(k):
                    t = 4 * u + k
                    act.wait_ge(pv_done, t + 1)
                    two_back(act, wo_done, u, k)
                    act.copy(head_hi[:, k % 2, :], headT_bank[:, :]).then_inc(head_hi_done, 1)

                if not has_next:
                    item("C1")
                    item("C2")
                    item("C3")
                    head_copy(0)
                    mix_query(0, 0)
                    exps(u, 2)
                    head_copy(1)
                    exps(u, 3)
                    mix_query(1, 1)
                    head_copy(2)
                    head_copy(3)
                    return

                item("K")
                item("Q0")
                head_copy(0)
                item("Q1")
                exps(u, 2)
                item("Q2")
                item("Q3")
                head_copy(1)
                item("C1")
                exps(u, 3)
                item("C2")
                if j == 0 and has_more:
                    split_w(v + 1, 0, proj_count(u, BODY.index("Q1")))
                item("C3")
                head_copy(2)
                if has_next:
                    exps(u + 1, 0)
                item("C0")
                if j == 1 and has_next:
                    split_wo(v + 1)
                head_copy(3)
                item("V")
                if j == 0 and has_more:
                    split_w(v + 1, 1, proj_count(u, BODY.index("V")))
                if has_next:
                    exps(u + 1, 1)


            def mix_query(b, j):
                act.wait_ge(x1T_done, b + 1)
                at_least(act, prod_done, b, 2)
                act.copy(qmix[:, j, :], mix_bank[:, 0:D]).then_inc(qmix_done, 1)

            def x2_copy(b, j):
                act.wait_ge(x2T_done, b + 1)
                act.copy(x2T[:, j, :], mix_bank[:, 0:D]).then_inc(x2copy_done, 1)

            def keep_x2(b, j):
                act.wait_ge(ln2[5], b + 1)
                act.copy(x[:, b, :], x2[:, j, :]).then_inc(x2_kept, 1)

            def gate_copy(b):
                act.wait_ge(gate_mm_done, b + 1)
                at_least(act, chosen_done, b, 1)
                act.copy(gate[:, :], tf_bank[:, D:D + FH]).then_inc(gate_done, 1)

            def query_hi(b, j):
                act.wait_ge(qT_done, b + 1)
                queries = tf_bank[:, 0:D].rearrange("p (n t) -> p n t", t=P)
                for r in range(2):
                    own = slice(CW * r, CW * (r + 1))
                    last = act.mul(qf[own, j, r::2, :], queries[own, :, :], FD ** -0.5)
                last.then_inc(qf_hi_done, 1)

            def gate_exp(b):
                act.wait_ge(gneg_done, b + 1)
                at_least(act, gprob_done, b, 1)
                act.activation(gexp[:, :], gate[:, :], ACT.Exp, bias=gneg[:, 0:1],
                               accum_out=gsum[:, 0:1]).then_inc(gexp_done, 1)

            def key_copy(b):
                act.wait_ge(ksT_done, b + 1)
                at_least(act, kblock_done, b, 1)
                act.copy(ksT[:, :], tf_bank[:, 0:P])
                act.copy(ksT_hi[:, :], tf_bank[:, 0:P]).then_inc(kscopy_done, 1)

            def fexps(b, c):
                act.wait_ge(fmax_done, 4 * b + c + 1)
                for h in range(4):
                    last = act.activation(prob[:, c % 2, h * P:(h + 1) * P],
                                          fscore_bank[c % 2][:, h * P:(h + 1) * P], ACT.Exp,
                                          bias=neg_max[:, c % 2, h:h + 1])
                last.then_inc(fexp_done, 1)

            def fprob_copy(b, c):
                act.wait_ge(fpt_done, 4 * b + c + 1)
                act.copy(probT[:, c % 2, :], fprobT_bank[c % 2][:, :]).then_inc(fptcopy_done, 1)

            phase_a(act, unit)

            x2_copy(0, 0)
            keep_x2(0, 0)
            gate_copy(0)
            mix_query(2, 0)
            gate_exp(0)
            key_copy(0)
            query_hi(0, 0)
            x2_copy(1, 1)
            mix_query(3, 1)
            keep_x2(1, 1)
            gate_copy(1)
            fexps(0, 0)
            gate_exp(1)
            fexps(0, 1)
            fprob_copy(0, 0)
            key_copy(1)

            def seq(b, j):
                if has(b, 1):
                    query_hi(b + 1, 1 - j)
                fexps(b, 2)
                fprob_copy(b, 1)
                if has(b, 2):
                    x2_copy(b + 2, j)
                if has(b, 4):
                    mix_query(b + 4, j)
                if has(b, 2):
                    keep_x2(b + 2, j)

                fexps(b, 3)
                fprob_copy(b, 2)
                if has(b, 2):
                    gate_copy(b + 2)

                if has(b, 1):
                    fexps(b + 1, 0)
                if has(b, 2):
                    gate_exp(b + 2)
                fprob_copy(b, 3)

                if has(b, 1):
                    fexps(b + 1, 1)
                if has(b, 2):
                    key_copy(b + 2)
                if has(b, 1):
                    fprob_copy(b + 1, 0)

            phase_b(act, seq)

        @block.vector
        def _(dve):
            def take_cos(u_next, j_next, name, bank_in):
                r, par = rope_count(u_next, name), rope_parity(j_next, name)
                dve.wait_ge(rot_done, r)
                if not (isinstance(r, int) and r <= 2):
                    dve.wait_ge(rope_done, r - 2)
                dve.tensor_tensor(t_cos[:, par, :].rearrange("p (b t) -> p b t", b=BH),
                                  bank_in[:, :].rearrange("p (b t) -> p b t", b=BH),
                                  cos[:, :].unsqueeze(1).to_broadcast([P, BH, P]),
                                  ALU.mult).then_inc(cos_done, 1)

            def add_sin(u_next, j_next, name):
                r, par = rope_count(u_next, name), rope_parity(j_next, name)
                if name == "K":
                    dst = k_rope[:, j_next % 2, :]
                else:
                    dst = q_rope[:, j_next % 2, int(name[1]), :]
                dve.wait_ge(cos_done, r)
                dve.wait_ge(sin_done, r)
                dve.tensor_tensor(dst, t_cos[:, par, :], t_sin[:, par, :], ALU.add
                                  ).then_inc(rope_done, 1)

            dve.memset(half_pow[:, :], -0.5)
            dve.memset(vext[:, :, FD:FD + 1], 1.0).then_inc(const_set, 1)

            def split_lo(lo, raw, hi, hi_ready, count, done):
                dve.wait_ge(hi_ready, count)
                dve.tensor_tensor(lo, raw, hi.bitcast(FP32), ALU.subtract).then_inc(done, 1)

            def split_w(g, part):
                cols = slice(part * 3 * P, (part + 1) * 3 * P)
                split_lo(w_lo[:, :, cols], w_raw[:, :, cols], w_hi[:, :, cols], w_hi_done,
                         2 * g + part + 1, w_lo_done)

            def add_skip(u, j):
                dve.wait_ge(in_toep[j], 8 * (u - j) + 16)
                for hh in range(2):
                    last = dve.scalar_tensor_tensor(toep[:, j, hh, 0:P], anti[:, :],
                                                    dcoef[:, bass.ds(2 * u + hh, 1)],
                                                    toep[:, j, hh, 0:P], ALU.mult, ALU.add)
                last.then_inc(toep_done, 1)

            split_lo(x_lo[:, 0, :, :], x_raw[:, :, :], x_hi[:, 0, :, :], x_hi_done, 1, x_lo_done)
            split_w(0, 0)
            split_w(0, 1)
            dve.wait_ge(in_trig, 32)
            for n, name in enumerate(ROPED):
                take_cos(0, 0, name, proj_bank[n % 2])
                if n >= 1:
                    add_sin(0, 0, ROPED[n - 1])
            add_sin(0, 0, ROPED[-1])
            dve.wait_ge(in_skip, 32)
            add_skip(0, 0)

            def row_max(u, k):
                t = 4 * u + k
                dve.wait_ge(scores_done, t + 1)
                dve.tensor_reduce(neg_max[:, k % 2, :],
                                  score_bank[k % 2][:, :].rearrange("p (h k) -> p h k", h=HG),
                                  axis=AX.X, op=ALU.max, negate=True).then_inc(max_done, 1)

            def invert(u, k):
                t = 4 * u + k
                dve.wait_ge(exp_done, t + 1)
                dve.reciprocal(rden[:, k % 2, :], den[:, k % 2, :]).then_inc(rden_done, 1)

            row_max(0, 0)
            split_lo(x_lo[:, 1, :, :], x_raw[:, :, :], x_hi[:, 1, :, :], x_hi_done, 2, x_lo_done)
            row_max(0, 1)
            invert(0, 0)
            invert(0, 1)

            def unit(v, j, has_next, has_more):
                u = 2 * v + j

                def cos_item(name):
                    if has_next:
                        take_cos(u + 1, j + 1, name, item_bank(BODY.index(name)))

                def add_item(name):
                    if has_next:
                        add_sin(u + 1, j + 1, name)

                def prob_copy(k):
                    t = 4 * u + k
                    dve.wait_ge(pt_done, t + 1)
                    two_back(dve, pv_done, u, k)
                    dve.tensor_copy(probT[:, k % 2, :], probT_bank[:, :]).then_inc(ptcopy_done, 1)

                def head_low(k):
                    t = 4 * u + k
                    dve.wait_ge(head_hi_done, t + 1)
                    dve.tensor_tensor(head_lo[:, k % 2, :], headT_bank[:, :],
                                      head_hi[:, k % 2, :].bitcast(FP32), ALU.subtract
                                      ).then_inc(head_lo_done, 1)

                def accumulate(a):
                    dve.wait_ge(wo_done, 4 * u + 2 * a + 2)
                    if a == 0:
                        dve.wait_ge(in_x, 16)
                    own = x[:, j * BH + 2 * a:j * BH + 2 * a + 2, :]
                    dve.tensor_tensor(own, acc_bank[a][:, :].rearrange("p (b n) -> p b n", b=2), own,
                                      ALU.add).then_inc(acc_done, 1)

                if not has_next:
                    prob_copy(0)
                    first_stats(0)
                    head_low(0)
                    row_max(u, 2)
                    first_apply(0, 0)
                    prob_copy(1)
                    row_max(u, 3)
                    invert(u, 2)
                    head_low(1)
                    dve.wait_ge(pv_done, 4 * u + 2)
                    first_apply(1, 1)
                    invert(u, 3)
                    prob_copy(2)
                    accumulate(0)
                    head_low(2)
                    prob_copy(3)
                    dve.wait_ge(in_ffn, 64)
                    dve.tensor_copy(causal[:, :], causal_raw[:, :])
                    dve.tensor_copy(identb[:, :], ident[:, :]).then_inc(mask_done, 1)
                    mix_sum(0, 0)
                    head_low(3)
                    accumulate(1)
                    return

                prob_copy(0)
                cos_item("K")
                add_item("K")
                head_low(0)
                cos_item("Q0")
                add_item("Q0")
                row_max(u, 2)
                cos_item("Q1")
                add_item("Q1")
                invert(u, 2)
                prob_copy(1)
                if has_next:
                    add_skip(u + 1, 1 - j)
                cos_item("Q2")
                add_item("Q2")
                head_low(1)
                cos_item("Q3")
                add_item("Q3")
                row_max(u, 3)
                accumulate(0)
                prob_copy(2)
                invert(u, 3)
                if j == 0 and has_more:
                    split_w(v + 1, 0)
                head_low(2)
                if has_next:
                    row_max(u + 1, 0)
                prob_copy(3)
                if has_next:
                    invert(u + 1, 0)
                head_low(3)
                if j == 0 and has_more:
                    split_w(v + 1, 1)
                if has_next:
                    row_max(u + 1, 1)
                accumulate(1)
                if has_next:
                    invert(u + 1, 1)


            def first_stats(s):
                dve.wait_ge(acc_done, 2 * (UNITS - 1 + s))
                for i in range(BH):
                    last = dve.bn_stats(stats[:, i, :], x[:, s * BH + i, :])
                last.then_inc(ln1[0], 1)
                dve.wait_ge(ln1[0], s + 1)
                for i in range(BH):
                    last = dve.bn_aggr(mean_var1[:, s * BH + i, :], stats[:, i, :])
                last.then_inc(ln1[1], 1)
                dve.wait_ge(ln1[1], s + 1)
                dve.tensor_scalar(var_eps1[:, s * BH:(s + 1) * BH], mean_var1[:, s * BH:(s + 1) * BH, 1],
                                  EPS, None, ALU.add).then_inc(ln1[2], 1)

            def first_apply(b, j):
                dve.wait_ge(ln1[3], b // BH + 1 if isinstance(b, int) else NS)
                at_least(dve, ln2[5], b, 2)
                dve.tensor_scalar(x1[:, j, :], x[:, b, :], mean_var1[:, b, 0:1], rstd1[:, bass.ds(b, 1)],
                                  ALU.subtract, ALU.mult).then_inc(ln1[4], 1)

            def norm_stats(n, ln, b, src):
                dve.wait_ge(ln[0], b + 1)
                dve.bn_stats(stats_of[n][:, :], src).then_inc(ln[1], 1)

            def norm_aggr(n, ln, b):
                dve.wait_ge(ln[1], b + 1)
                dve.memset(carrier[:, :], 0.0)
                dve.bn_aggr(mean_var_of[n][:, :], stats_of[n][:, :]).then_inc(ln[2], 1)

            def norm_eps(n, ln, b):
                dve.wait_ge(ln[2], b + 1)
                dve.tensor_scalar(var_eps_of[n][:, :], mean_var_of[n][:, 1:2], EPS, None, ALU.add
                                  ).then_inc(ln[3], 1)

            def norm_apply(n, ln, b, src, out):
                dve.wait_ge(ln[4], b + 1)
                dve.tensor_scalar(out, src, mean_var_of[n][:, 0:1], rstd_of[n][:, 0:1],
                                  ALU.subtract, ALU.mult).then_inc(ln[5], 1)

            def second_apply(b, j):
                at_least(dve, x2_kept, b, 2)
                norm_apply(0, ln2, b, x1[:, j, :], x2[:, j, :])

            def mix_sum(b, j):
                dve.wait_ge(prod_done, b + 1)
                at_least(dve, mix_done, b, 2)
                dve.tensor_reduce(mixT[:, j, :], prod[:, j, :, :, :], axis=AX.X, op=ALU.add
                                  ).then_inc(mixT_done, 1)

            def add_mix(b, j):
                dve.wait_ge(mix_done, b + 1)
                dve.wait_ge(ln1[4], b + 1)
                dve.tensor_tensor(x1[:, j, :], mix_bank[:, 0:D], x1[:, j, :], ALU.add).then_inc(ln2[0], 1)

            def mix_norm(b, j):
                add_mix(b, j)
                norm_stats(0, ln2, b, x1[:, j, :])
                norm_aggr(0, ln2, b)
                norm_eps(0, ln2, b)
                second_apply(b, j)

            def gating(b):
                dve.wait_ge(gate_done, b + 1)
                at_least(dve, gexp_done, b, 1)
                dve.tensor_reduce(gtop[:, 0:1], gate[:, :], axis=AX.X, op=ALU.max).then_inc(gtop_done, 1)
                dve.tensor_reduce(gneg[:, 0:1], gate[:, :], axis=AX.X, op=ALU.max, negate=True
                                  ).then_inc(gneg_done, 1)
                dve.wait_ge(gtop_done, b + 1)
                dve.scalar_tensor_tensor(gscore[:, :], gate[:, :], gtop[:, 0:1], ties[:, :],
                                         ALU.is_equal, ALU.mult).then_inc(gscore_done, 1)
                dve.wait_ge(gscore_done, b + 1)
                dve.tensor_reduce(gbest[:, 0:1], gscore[:, :], axis=AX.X, op=ALU.max
                                  ).then_inc(gbest_done, 1)
                dve.wait_ge(gbest_done, b + 1)
                dve.tensor_scalar(chosen[:, :], gscore[:, :], gbest[:, 0:1], None, ALU.is_equal
                                  ).then_inc(chosen_done, 1)

            def query_lo(b, j):
                dve.wait_ge(qf_hi_done, b + 1)
                queries = tf_bank[:, 0:D].rearrange("p (n t) -> p n t", t=P)
                for r in range(2):
                    own, other = slice(CW * r, CW * (r + 1)), slice(CW * (1 - r), CW * (2 - r))
                    last = dve.scalar_tensor_tensor(qf[other, j, r::2, :], queries[own, :, :], FD ** -0.5,
                                                    qf[own, j, r::2, :].bitcast(FP32),
                                                    ALU.mult, ALU.subtract)
                last.then_inc(qf_lo_done, 1)

            def share(b):
                dve.wait_ge(chosen_done, b + 1)
                dve.wait_ge(kvf_done, b + 1)
                dve.tensor_tensor(kv_masked[:, :, :, :],
                                  kvf_bank[:, :].rearrange("p (n h d) -> p n h d", n=2, h=FH),
                                  chosen[:, :].unsqueeze(1).unsqueeze(3).to_broadcast([P, 2, FH, FD]),
                                  ALU.mult).then_inc(masked_done, 1)
                dve.wait_ge(gexp_done, b + 1)
                dve.reciprocal(gprob[:, 0:1], gsum[:, 0:1]).then_inc(gprob_done, 1)
                dve.wait_ge(masked_done, b + 1)
                dve.tensor_reduce(kv_shared[:, :, :],
                                  kv_masked[:, :, :, :].rearrange("p n h d -> p n d h"),
                                  axis=AX.X, op=ALU.add).then_inc(shared_done, 1)
                dve.wait_ge(shared_done, b + 1)
                at_least(dve, ksT_done, b, 1)
                dve.tensor_copy(krep[:, :, :], kv_shared[:, 0, :].unsqueeze(1).to_broadcast([P, FB, FD])
                                ).then_inc(krep_done, 1)
                dve.wait_ge(gprob_done, b + 1)
                dve.tensor_scalar(vext[:, b, 0:FD], kv_shared[:, 1, :], gprob[:, 0:1], None, ALU.mult
                                  ).then_inc(vext_done, 1)

            def frow_max(b, c):
                dve.wait_ge(fscores_done, 4 * b + c + 1)
                dve.tensor_reduce(neg_max[:, c % 2, :],
                                  fscore_bank[c % 2][:, :].rearrange("p (h k) -> p h k", h=4),
                                  axis=AX.X, op=ALU.max, negate=True).then_inc(fmax_done, 1)

            y = y_bank[:, 0:FH * (FD + 1)].rearrange("p (h d) -> p h d", h=FH)

            y_flat = ynorm[:, :, :].rearrange("p h d -> p (h d)")

            def y_invert(b):
                dve.wait_ge(y_done, 4 * b + 4)
                dve.reciprocal(yden[:, :], y[:, :, FD]).then_inc(yden_done, 1)

            def y_scale(b):
                dve.wait_ge(yden_done, b + 1)
                dve.tensor_tensor(ynorm[:, :, :], y[:, :, 0:FD],
                                  yden[:, :].unsqueeze(2).to_broadcast([P, FH, FD]), ALU.mult
                                  ).then_inc(ynorm_done, 1)

            def add_ffn(b):
                dve.wait_ge(ynorm_done, b + 1)
                dve.wait_ge(x2_kept, b + 1)
                dve.tensor_tensor(y_flat, y_flat, x[:, b, :],
                                  ALU.add).then_inc(ln3[0], 1)

            phase_a(dve, unit)

            mix_norm(0, 0)
            first_apply(2, 0)
            gating(0)
            mix_sum(1, 1)
            share(0)
            mix_norm(1, 1)
            first_apply(3, 1)
            query_lo(0, 0)
            gating(1)
            frow_max(0, 0)
            frow_max(0, 1)
            mix_sum(2, 0)
            share(1)
            mix_norm(2, 0)
            frow_max(0, 2)
            first_stats(1)
            query_lo(1, 1)

            def seq(b, j):
                if has(b, 4):
                    first_apply(b + 4, j)
                frow_max(b, 3)
                if has(b, 3):
                    mix_sum(b + 3, 1 - j)

                if has(b, 1):
                    frow_max(b + 1, 0)
                if has(b, 2):
                    gating(b + 2)
                    share(b + 2)
                if has(b, 1):
                    frow_max(b + 1, 1)

                if has(b, 3):
                    add_mix(b + 3, 1 - j)
                    norm_stats(0, ln2, b + 3, x1[:, 1 - j, :])
                y_invert(b)
                if has(b, 3):
                    norm_aggr(0, ln2, b + 3)
                y_scale(b)
                if has(b, 3):
                    norm_eps(0, ln2, b + 3)
                add_ffn(b)
                norm_stats(1, ln3, b, y_flat)
                if has(b, 1):
                    frow_max(b + 1, 2)
                norm_aggr(1, ln3, b)
                if has(b, 3):
                    second_apply(b + 3, 1 - j)
                norm_eps(1, ln3, b)
                if has(b, 2):
                    query_lo(b + 2, j)
                norm_apply(1, ln3, b, y_flat, x[:, b, :])

            phase_b(dve, seq)

        @block.gpsimd
        def _(pool):
            def pairs(u_next, head, buf):
                if not (isinstance(u_next, int) and u_next <= 1):
                    pool.wait_ge(proj_done, proj_count(u_next - 2, BODY.index("C3")))
                src = ctxT[:, :, bass.ds(head * NB, 2 * NB), :]
                for d in range(HD):
                    at, n = PAIR_AT[d], HD - d
                    last = pool.tensor_tensor(kv[:, buf, :, :, at:at + n], src[:, :, :, 0:n],
                                              src[:, :, :, d:HD], ALU.mult)
                last.then_inc(kv_done, 1)

            def times_sin(u_next, j_next, name):
                r, par = rope_count(u_next, name), rope_parity(j_next, name)
                pool.wait_ge(rot_done, r)
                if not (isinstance(r, int) and r <= 2):
                    pool.wait_ge(rope_done, r - 2)
                pool.tensor_tensor(t_sin[:, par, :].rearrange("p (b t) -> p b t", b=BH),
                                   rot[:, par, :].rearrange("p (b t) -> p b t", b=BH),
                                   sin[:, :].unsqueeze(1).to_broadcast([P, BH, P]), ALU.mult
                                   ).then_inc(sin_done, 1)

            pool.wait_ge(in_ctx, 16)
            pairs(0, 0, 0)
            pool.wait_ge(in_trig, 32)
            for name in ROPED:
                times_sin(0, 0, name)

            def split_wo(g):
                pool.wait_ge(wo_hi_done, g + 1)
                heads = bass.ds(HG * g, HG)
                pool.tensor_tensor(wo_lo[:, heads, :], wo_raw[:, :, :], wo_hi[:, heads, :].bitcast(FP32),
                                   ALU.subtract).then_inc(wo_lo_done, 1)

            def normalize(u, k):
                pool.wait_ge(rden_done, 4 * u + k + 1)
                own = prob[:, k % 2, :].rearrange("p (h k) -> p h k", h=HG)
                pool.tensor_tensor(own, own, rden[:, k % 2, :].unsqueeze(2).to_broadcast([P, HG, P]),
                                   ALU.mult).then_inc(norm_done, 1)

            split_wo(0)
            normalize(0, 0)
            normalize(0, 1)

            def unit(v, j, has_next, has_more):
                u = 2 * v + j

                def sin_item(name):
                    if has_next:
                        times_sin(u + 1, j + 1, name)

                if not has_next:
                    pool.wait_ge(const_set, 1)
                    power(rstd1[:, 0:BH], var_eps1[:, 0:BH], ln1, 1)
                    pool.wait_ge(conv_done, CONV * UNITS)
                    products(0, 0, NEAR)
                    normalize(u, 2)
                    normalize(u, 3)
                    products(0, 0, FAR)
                    return

                sin_item("K")
                sin_item("Q0")
                sin_item("Q1")
                normalize(u, 2)
                sin_item("Q2")
                sin_item("Q3")
                if has_next:
                    pairs(u + 1, 4 * v + 2 * j + 2, 1 - j)
                normalize(u, 3)
                if has_next:
                    normalize(u + 1, 0)
                if j == 1 and has_next:
                    split_wo(v + 1)
                if has_next:
                    normalize(u + 1, 1)


            def second_power(b):
                power(rstd_of[0][:, :], var_eps_of[0][:, :], ln2, b + 1)

            NEAR, FAR = range(0, HD // 2), range(HD // 2, HD)

            def products(b, j, distances):
                if distances[0] == 0:
                    pool.wait_ge(qmix_done, b + 1)
                    at_least(pool, mixT_done, b, 2)
                q = qmix[:, j, :].rearrange("p (a i) -> p a i", i=HD)
                pr = prod[:, j, :, :, :].rearrange("p a j i -> p a (j i)")
                y = y36[:, b, :, :, :].rearrange("p c h n -> p (c h) n")
                for d in distances:
                    at, n = PAIR_AT[d], HD - d
                    last = pool.tensor_tensor(pr[:, :, d * HD:d * HD + (n - 1) * (HD + 1) + 1:HD + 1],
                                              y[:, :, at:at + n], q[:, :, 0:n], ALU.mult)
                    if d:
                        last = pool.tensor_tensor(pr[:, :, d:d + (n - 1) * (HD + 1) + 1:HD + 1],
                                                  y[:, :, at:at + n], q[:, :, d:HD], ALU.mult)
                if distances[-1] == HD - 1:
                    last.then_inc(prod_done, 1)

            def block_keys(b, j):
                mask = blocks[:, :].unsqueeze(2).to_broadcast([P, FC, P])
                pool.wait_ge(kscopy_done, b + 1)
                pool.tensor_tensor(ksT_lo[:, :], ksT[:, :], ksT_hi[:, :].bitcast(FP32), ALU.subtract
                                   ).then_inc(ks_lo_done, 1)
                pool.tensor_tensor(kblock[:, j, 0, :, :],
                                   ksT_hi[:, :].bitcast(FP32).unsqueeze(1).to_broadcast([P, FC, P]),
                                   mask, ALU.mult)
                pool.wait_ge(ks_lo_done, b + 1)
                pool.tensor_tensor(kblock[:, j, 1, :, :],
                                   ksT_lo[:, :].bitcast(FP32).unsqueeze(1).to_broadcast([P, FC, P]),
                                   mask, ALU.mult).then_inc(kblock_done, 1)

            def power(dst, src, ln, count):
                pool.wait_ge(ln[-3], count)
                pool.tensor_tensor(dst, src, half_pow[:, 0:dst.shape[1]], ALU.pow).then_inc(ln[-2], 1)

            phase_a(pool, unit)

            products(1, 1, NEAR)
            second_power(0)
            products(1, 1, FAR)
            products(2, 0, NEAR)
            products(2, 0, FAR)
            second_power(1)
            pool.wait_ge(in_ffn, 64)
            block_keys(0, 0)
            products(3, 1, NEAR)
            products(3, 1, FAR)
            second_power(2)
            power(rstd1[:, BH:NB], var_eps1[:, BH:NB], ln1, 2)
            block_keys(1, 1)

            def seq(b, j):
                if has(b, 4):
                    products(b + 4, j, NEAR)
                    products(b + 4, j, FAR)
                if has(b, 3):
                    second_power(b + 3)
                power(rstd_of[1][:, :], var_eps_of[1][:, :], ln3, b + 1)
                if has(b, 2):
                    block_keys(b + 2, j)

            phase_b(pool, seq)


def _layouts(a):
    import numpy as np
    f = np.float32
    x = np.asarray(a["x"]).reshape(NB * P, D)
    L = {}
    L["xt"] = x.T.reshape(C, P, NS, TOK).transpose(1, 2, 0, 3)
    L["x"] = x.reshape(NB, P, D).transpose(1, 0, 2)
    wq = np.asarray(a["L0_attn_Wq"]).reshape(NG, HG * P, D)
    wk = np.asarray(a["L0_attn_Wk"]).reshape(NG, P, D)
    wv = np.asarray(a["L0_attn_Wv"]).reshape(NG, P, D)
    w = np.concatenate([wk, wq, wv], axis=1)
    L["wqkv"] = w.transpose(0, 2, 1).reshape(NG, C, P, 6 * P).transpose(2, 0, 1, 3)
    L["wo"] = np.asarray(a["L0_attn_Wo"]).T.reshape(NH, P, D).transpose(1, 0, 2)
    filt = np.asarray(a["L0_xattn_ssm_kernel"])
    padded = np.concatenate([np.zeros((XH, P - 1), f), filt], axis=1)
    L["toep"] = np.stack([padded[:, p:p + D] for p in range(P)])
    L["dcoef"] = np.broadcast_to(np.asarray(a["L0_xattn_D"])[None, :], (P, XH))
    c = np.asarray(a["ctx_2048"]).reshape(NB, XH, HD, C, P)[..., ::-1]
    L["ctx"] = c.transpose(4, 3, 1, 0, 2).reshape(P, C, XH * NB, HD)
    wf = np.concatenate([np.asarray(a["L0_ffn_W_qkv"]), np.asarray(a["L0_ffn_W_gate"])], axis=0)
    L["wf"] = wf.T.reshape(C, P, 3 * D + FH).transpose(1, 0, 2)
    inv = (f(1.0) / f(10000.0) ** (np.arange(0, P, 2, dtype=f) / f(P))).astype(f)
    angle = np.repeat(np.arange(P, dtype=f)[:, None] * inv[None, :], 2, axis=1).T
    root = float(P) ** -0.25
    sign = np.where(np.arange(P) < P // 2, -1.0, 1.0)[:, None]
    L["cos"] = (np.cos(angle).astype(np.float64) * root).astype(f)
    L["sin"] = (np.sin(angle).astype(np.float64) * root * sign).astype(f)
    L["ident"] = np.eye(P, dtype=f)
    L["anti"] = np.eye(P, dtype=f)[::-1]
    L["causal"] = np.where(np.tril(np.ones((P, P))) > 0, 0.0, -1e30).astype(f)
    L["blocks"] = (np.arange(P)[:, None] % CW // FD == np.arange(FC)[None, :]).astype(f)
    L["ties"] = np.broadcast_to(np.arange(FH, 0, -1).astype(f)[None, :], (P, FH))
    return {k: np.ascontiguousarray(v) for k, v in L.items()}


def kernel(**inputs):
    import concourse.bacc as bacc
    from concourse.bass_utils import run_bass_kernel_spmd
    nc = bacc.Bacc("TRN2", target_bir_lowering=False, num_devices=1)
    arrays, args = {}, []
    for name, a in _layouts(inputs).items():
        arrays[f"in_{name}"] = a
        args.append(nc.dram_tensor(f"in_{name}", a.shape, mybir.dt.from_np(a.dtype),
                                   kind="ExternalInput").ap())
    out = nc.dram_tensor("out", (NB, P, D), FP32, kind="ExternalOutput").ap()
    decoder_kernel(nc, *args, out)
    result = run_bass_kernel_spmd(nc, [arrays], core_ids=[0])
    return result.results[0]["out"]
```

```python
import concourse.bass as bass
from concourse import mybir
from contextlib import ExitStack

FP32 = mybir.dt.float32
BF16 = mybir.dt.bfloat16
FP32R = mybir.dt.float32r
ALU = mybir.AluOpType
ACT = mybir.ActivationFunctionType
AX = mybir.AxisListType

P = 128
NB = 8
D = 256
C = D // P
NG = 4
HG = 4
NH = NG * HG
NS = 2
BH = NB // NS
TOK = BH * P
UNITS = NG * NS
XH = 16
HD = 8
NPAIR = HD * (HD + 1) // 2
PAIR_AT = [sum(HD - e for e in range(d)) for d in range(HD)]
FH = 16
FD = 16
FB = P // FD
FC = 4
CW = FC * FD
EPS = 1e-5
CONV = 4

COLS = ["K", "Q0", "Q1", "Q2", "Q3", "V"]
FRONT = ["K", "Q0", "Q1", "Q2", "Q3", "V", "C0"]
BODY = ["K", "Q0", "Q1", "Q2", "Q3", "C1", "C2", "C3", "C0", "V"]
LAST = ["C1", "C2", "C3"]
ROPED = ["K", "Q0", "Q1", "Q2", "Q3"]


def decoder_kernel(nc, xt_d, x_d, wqkv_d, wo_d, toep_d, dcoef_d, ctx_d, wf_d, cos_d, sin_d, ident_d,
                   anti_d, causal_d, blocks_d, ties_d, out_d):
    ctx = ExitStack()
    with ctx:
        def sb(name, shape, dt=FP32):
            return ctx.enter_context(nc.sbuf_tensor(name, shape, dt))

        def sem(name):
            return ctx.enter_context(nc.semaphore(name))

        x_raw = sb("x_raw", [P, C, TOK])
        x_hi = sb("x_hi", [P, NS, C, TOK], FP32R)
        x_lo = sb("x_lo", [P, NS, C, TOK], FP32R)
        x = sb("x", [P, NB, D])
        w_raw = sb("w_raw", [P, C, 6 * P])
        w_hi = sb("w_hi", [P, C, 6 * P], FP32R)
        w_lo = sb("w_lo", [P, C, 6 * P], FP32R)
        wo_raw = sb("wo_raw", [P, HG, D])
        wo_hi = sb("wo_hi", [P, NH, D], FP32R)
        wo_lo = sb("wo_lo", [P, NH, D], FP32R)
        toep = sb("toep", [P, 2, 2, D])
        dcoef = sb("dcoef", [P, XH])
        ctxT = sb("ctxT", [P, C, XH * NB, HD])
        kv = sb("kv", [P, 2, C, 2 * NB, NPAIR])
        y36 = sb("y36", [P, NB, C, XH, NPAIR])
        cos = sb("cos", [P, P])
        sin = sb("sin", [P, P])
        ident = sb("ident", [P, P])
        anti = sb("anti", [P, P])
        identb = sb("identb", [P, P], BF16)
        causal_raw = sb("causal_raw", [P, P])
        causal = sb("causal", [P, P], BF16)
        blocks = sb("blocks", [P, FC])
        ties = sb("ties", [P, FH])
        q_rope = sb("q_rope", [P, 2, HG, TOK])
        k_rope = sb("k_rope", [P, 2, TOK])
        vT = sb("vT", [P, TOK])
        v_tok = sb("v_tok", [P, 2, TOK])
        rot = sb("rot", [P, 2, TOK])
        t_cos = sb("t_cos", [P, 2, TOK])
        t_sin = sb("t_sin", [P, 2, TOK])
        neg_max = sb("neg_max", [P, 2, HG])
        den = sb("den", [P, 2, HG])
        rden = sb("rden", [P, 2, HG])
        prob = sb("prob", [P, 2, HG * P])
        probT = sb("probT", [P, 2, HG * P])
        head_hi = sb("head_hi", [P, 2, HG * P], FP32R)
        head_lo = sb("head_lo", [P, 2, HG * P], FP32R)
        stats = sb("stats", [P, BH, 6])
        mean_var1 = sb("mean_var1", [P, NB, 2])
        rstd1 = sb("rstd1", [P, NB])
        stats_of = [sb(f"stats{n}", [P, 6]) for n in (2, 3)]
        mean_var_of = [sb(f"mean_var{n}", [P, 2]) for n in (2, 3)]
        var_eps1 = sb("var_eps1", [P, NB])
        var_eps_of = [sb(f"var_eps{n}", [P, 1]) for n in (2, 3)]
        rstd_of = [sb(f"rstd{n}", [P, 1]) for n in (2, 3)]
        half_pow = sb("half_pow", [P, BH])
        carrier = sb("carrier", [P, 1])
        prod = q_rope[:, :, :, :].rearrange("p n h t -> p n (h t)").rearrange(
            "p n (a j i) -> p n a j i", j=HD, i=HD)
        kblock = x_hi[:, :, :, :].rearrange("p j n (h k) -> p j n h k", k=P)
        wf = sb("wf", [P, C, 3 * D + FH])
        qmix = rot[:, :, 0:D]
        mixT = t_cos[:, :, 0:D]
        x1 = v_tok[:, :, 0:D]
        x2 = v_tok[:, :, D:2 * D]
        x2T = k_rope[:, :, 0:D]
        qf = w_hi[:, :, 0:FC * P].rearrange("p j (c t) -> p j c t", t=P)
        gate = sb("gate", [P, FH])
        gexp = sb("gexp", [P, FH])
        gtop = sb("gtop", [P, 1])
        gneg = sb("gneg", [P, 1])
        gsum = sb("gsum", [P, 1])
        gprob = sb("gprob", [P, 1])
        gscore = sb("gscore", [P, FH])
        gbest = sb("gbest", [P, 1])
        chosen = sb("chosen", [P, FH])
        kv_masked = x_raw[:, 0, :].rearrange("p (n h d) -> p n h d", n=2, h=FH)
        kv_shared = sb("kv_shared", [P, 2, FD])
        krep = x_raw[:, 1, 0:P].rearrange("p (h d) -> p h d", d=FD)
        ksT = x_raw[:, 1, P:2 * P]
        ksT_hi = sb("ksT_hi", [P, P], FP32R)
        ksT_lo = sb("ksT_lo", [P, P], FP32R)
        vext = sb("vext", [P, NB, FD + 1])
        yden = sb("yden", [P, FH])
        ynorm = x_raw[:, 1, 2 * P:4 * P].rearrange("p (h d) -> p h d", d=FD)

        bank = [ctx.enter_context(nc.psum_tensor(f"bank{i}", [P, 512], FP32)) for i in range(8)]
        proj_bank = [bank[0], bank[1]]
        score_bank = [bank[2], bank[3]]
        probT_bank, headT_bank = bank[4], bank[5]
        acc_bank = [bank[6], bank[7]]
        front_bank = dict(zip(FRONT, [bank[0], bank[1], bank[6], bank[7], bank[4], bank[0], bank[1]]))
        fscore_bank = [bank[4], bank[5]]
        fprobT_bank = [bank[2], bank[3]]
        mix_bank, tf_bank, kvf_bank, y_bank = bank[0], bank[1], bank[6], bank[7]

        in_xt = sem("in_xt")
        x_hi_done = sem("x_hi_done")
        x_lo_done = sem("x_lo_done")
        w_hi_done = sem("w_hi_done")
        w_lo_done = sem("w_lo_done")
        wo_hi_done = sem("wo_hi_done")
        wo_lo_done = sem("wo_lo_done")
        in_w_first = sem("in_w_first")
        in_w = sem("in_w")
        in_wo = sem("in_wo")
        in_trig = sem("in_trig")
        in_ident = sem("in_ident")
        in_toep = [sem("in_toep0"), sem("in_toep1")]
        in_skip = sem("in_skip")
        in_ctx = sem("in_ctx")
        in_x = sem("in_x")
        in_ffn = sem("in_ffn")
        mask_done = sem("mask_done")
        const_set = sem("const_set")
        toep_done = sem("toep_done")
        proj_done = sem("proj_done")
        rot_done = sem("rot_done")
        cos_done = sem("cos_done")
        sin_done = sem("sin_done")
        rope_done = sem("rope_done")
        vT_done = sem("vT_done")
        v_turned = sem("v_turned")
        v_done = sem("v_done")
        conv_done = sem("conv_done")
        kv_done = sem("kv_done")
        scores_done = sem("scores_done")
        max_done = sem("max_done")
        exp_done = sem("exp_done")
        rden_done = sem("rden_done")
        norm_done = sem("norm_done")
        pt_done = sem("pt_done")
        ptcopy_done = sem("ptcopy_done")
        pv_done = sem("pv_done")
        head_hi_done = sem("head_hi_done")
        head_lo_done = sem("head_lo_done")
        wo_done = sem("wo_done")
        acc_done = sem("acc_done")
        ln1 = [sem(f"ln1_{n}") for n in ("stats", "aggr", "eps", "rstd", "out")]
        ln2 = [sem(f"ln2_{n}") for n in ("sum", "stats", "aggr", "eps", "rstd", "out")]
        ln3 = [sem(f"ln3_{n}") for n in ("sum", "stats", "aggr", "eps", "rstd", "out")]
        x1T_done = sem("x1T_done")
        qmix_done = sem("qmix_done")
        prod_done = sem("prod_done")
        near_done = sem("near_done")
        mixT_done = sem("mixT_done")
        mix_done = sem("mix_done")
        x2T_done = sem("x2T_done")
        x2_kept = sem("x2_kept")
        x2copy_done = sem("x2copy_done")
        gate_mm_done = sem("gate_mm_done")
        gate_done = sem("gate_done")
        kvf_done = sem("kvf_done")
        qT_done = sem("qT_done")
        qf_hi_done = sem("qf_hi_done")
        qf_lo_done = sem("qf_lo_done")
        gtop_done = sem("gtop_done")
        gneg_done = sem("gneg_done")
        gexp_done = sem("gexp_done")
        gprob_done = sem("gprob_done")
        gscore_done = sem("gscore_done")
        gbest_done = sem("gbest_done")
        chosen_done = sem("chosen_done")
        masked_done = sem("masked_done")
        shared_done = sem("shared_done")
        krep_done = sem("krep_done")
        vext_done = sem("vext_done")
        ksT_done = sem("ksT_done")
        kscopy_done = sem("kscopy_done")
        ks_lo_done = sem("ks_lo_done")
        kblock_lo_done = sem("kblock_lo_done")
        kblock_hi_done = sem("kblock_hi_done")
        fscores_done = sem("fscores_done")
        fmax_done = sem("fmax_done")
        fexp_done = sem("fexp_done")
        fpt_done = sem("fpt_done")
        fptcopy_done = sem("fptcopy_done")
        y_done = sem("y_done")
        yden_done = sem("yden_done")
        ynorm_done = sem("ynorm_done")
        stored = sem("stored")

        def proj_count(u, i):
            return len(FRONT) + len(BODY) * u + i + 1

        def item_bank(i):
            return proj_bank[(len(FRONT) + i) % 2]

        def rope_count(u_next, name):
            return len(ROPED) * u_next + ROPED.index(name) + 1

        def rope_parity(j_next, name):
            return (len(ROPED) * j_next + ROPED.index(name)) % 2

        def two_back(eng, done, n, k):
            if k >= 2:
                eng.wait_ge(done, 4 * n + k - 1)

        def at_least(eng, done, n, back):
            if not (isinstance(n, int) and n < back):
                eng.wait_ge(done, n - back + 1)

        block = ctx.enter_context(nc.Block())

        def phase_a(eng, unit):
            with eng.Fori(0, NG - 1, 1) as v:
                unit(v, 0, True, True)
                unit(v, 1, True, True)
            unit(NG - 1, 0, True, False)
            unit(NG - 1, 1, False, False)

        def phase_b(eng, seq, last_seq):
            with eng.Fori(0, NB // 2 - 2, 1) as w:
                seq(2 * w, 0)
                seq(2 * w + 1, 1)
            for b in range(NB - 4, NB):
                last_seq(b, b % 2)

        NEAR, FAR = range(0, HD // 2), range(HD // 2, HD)

        def pair_products(eng, b, j, distances):
            q = qmix[:, j, :].rearrange("p (a i) -> p a i", i=HD)
            pr = prod[:, j, :, :, :].rearrange("p a j i -> p a (j i)")
            y = y36[:, b, :, :, :].rearrange("p c h n -> p (c h) n")
            for d in distances:
                at, n = PAIR_AT[d], HD - d
                last = eng.tensor_tensor(pr[:, :, d * HD:d * HD + (n - 1) * (HD + 1) + 1:HD + 1],
                                         y[:, :, at:at + n], q[:, :, 0:n], ALU.mult)
                if d:
                    last = eng.tensor_tensor(pr[:, :, d:d + (n - 1) * (HD + 1) + 1:HD + 1],
                                             y[:, :, at:at + n], q[:, :, d:HD], ALU.mult)
            return last

        @block.sync
        def _(sp):
            def load_toep(u, j):
                if not (isinstance(u, int) and u <= 1):
                    sp.wait_ge(proj_done, proj_count(u - 2, BODY.index("C3")))
                sp.dma_start(toep[:, j, :, :], toep_d[:, bass.ds(2 * u, 2), :]).then_inc(in_toep[j], 16)

            sp.dma_start(x_raw[:, :, :], xt_d[:, 0, :, :]).then_inc(in_xt, 16)
            sp.dma_start(cos[:, :], cos_d).then_inc(in_trig, 16)
            sp.dma_start(sin[:, :], sin_d).then_inc(in_trig, 16)
            sp.dma_start(ctxT[:, :, :, :], ctx_d).then_inc(in_ctx, 16)
            load_toep(0, 0)
            sp.dma_start(dcoef[:, :], dcoef_d).then_inc(in_skip, 16)
            sp.dma_start(anti[:, :], anti_d).then_inc(in_skip, 16)
            sp.dma_start(ident[:, :], ident_d).then_inc(in_ident, 16)
            sp.wait_ge(x_lo_done, 1)
            sp.dma_start(x_raw[:, :, :], xt_d[:, 1, :, :]).then_inc(in_xt, 16)
            sp.dma_start(wo_raw[:, :, :], wo_d[:, 0:HG, :]).then_inc(in_wo, 16)
            load_toep(1, 1)
            sp.dma_start(x[:, :, :], x_d).then_inc(in_x, 16)
            with sp.Fori(0, NG - 1, 1) as v:
                sp.wait_ge(w_lo_done, 2 * v + 2)
                sp.dma_start(w_raw[:, :, :], wqkv_d[:, v + 1, :, :]).then_inc(in_w, 16)
                sp.wait_ge(wo_lo_done, v + 1)
                sp.dma_start(wo_raw[:, :, :], wo_d[:, bass.ds(HG * v + HG, HG), :]).then_inc(in_wo, 16)
                load_toep(2 * v + 2, 0)
                load_toep(2 * v + 3, 1)
            sp.dma_start(wf[:, :, :], wf_d).then_inc(in_ffn, 16)
            sp.dma_start(causal_raw[:, :], causal_d).then_inc(in_ffn, 16)
            sp.dma_start(blocks[:, :], blocks_d).then_inc(in_ffn, 16)
            sp.dma_start(ties[:, :], ties_d).then_inc(in_ffn, 16)

            with sp.Fori(0, NB, 1) as b:
                sp.wait_ge(ln3[5], b + 1)
                sp.dma_start(out_d[b, :, :], x[:, b, :]).then_inc(stored, 16)
            sp.wait_ge(stored, 16 * NB)

        @block.tensor
        def _(pe):
            def project(j, name, out, first=False):
                col = COLS.index(name) * P
                for n, (wp, xp) in enumerate(((w_hi, x_hi), (w_hi, x_lo), (w_lo, x_hi))):
                    if first and n == 1:
                        pe.wait_ge(x_lo_done, 1)
                    if first and n == 2:
                        pe.wait_ge(w_lo_done, 1)
                    for c in range(C):
                        last = pe.matmul(out[:, :], wp[:, c, col:col + P], xp[:, j, c, :],
                                         start=(c + n == 0), stop=(c == C - 1 and n == 2))
                last.then_inc(proj_done, 1)

            def v_turn(u_next, out):
                pe.wait_ge(vT_done, u_next + 1)
                for b in range(BH):
                    last = pe.transpose(out[:, b * P:(b + 1) * P], vT[:, b * P:(b + 1) * P], ident[:, :])
                last.then_inc(v_turned, 1)

            def conv(j, i, bank_out):
                hh, lb = i // 2, i % 2
                out = bank_out[:, 0:NB * NPAIR]
                for m in range(lb + 1):
                    tap = (lb - m) * P
                    last = pe.matmul(out, toep[:, j, hh, tap:tap + P],
                                     kv[:, j, m, hh * NB:(hh + 1) * NB, :],
                                     start=(m == 0), stop=(m == lb))
                last.then_inc(proj_done, 1)

            def scores(u, j, k):
                if k == 0:
                    pe.wait_ge(rope_done, len(ROPED) * (u + 1))
                if isinstance(u, int) and 4 * u + k < 2:
                    pass
                else:
                    pe.wait_ge(exp_done, 4 * u + k - 1)
                for h in range(HG):
                    last = pe.matmul(score_bank[k % 2][:, h * P:(h + 1) * P],
                                     q_rope[:, j, h, k * P:(k + 1) * P],
                                     k_rope[:, j, k * P:(k + 1) * P], start=True, stop=True)
                last.then_inc(scores_done, 1)

            pe.wait_ge(x_hi_done, 1)
            pe.wait_ge(w_hi_done, 1)
            for name in COLS:
                if name == "V":
                    pe.wait_ge(cos_done, 1)
                if name == "Q2":
                    pe.wait_ge(w_lo_done, 2)
                project(0, name, front_bank[name], first=(name == "K"))
            scores(0, 0, 0)
            pe.wait_ge(in_ident, 16)
            v_turn(0, front_bank["V"])
            scores(0, 0, 1)
            pe.wait_ge(cos_done, 2)
            pe.wait_ge(kv_done, 1)
            pe.wait_ge(toep_done, 1)
            conv(0, 0, front_bank["C0"])

            def bank_free(u, items, i):
                if i >= 2:
                    name, un = items[i - 2], u + 1
                else:
                    name, un = BODY[len(BODY) - 2 + i], u
                if name == "V":
                    pe.wait_ge(v_done, un + 1)
                elif name == "C0":
                    pe.wait_ge(conv_done, CONV * un + 1)
                elif name[0] == "C":
                    pe.wait_ge(conv_done, CONV * u + int(name[1]) + 1)
                else:
                    pe.wait_ge(cos_done, rope_count(un, name))

            def unit(v, j, has_next, has_more):
                u = 2 * v + j
                items = BODY if has_next else LAST

                def item(name):
                    if name not in items:
                        return
                    i = items.index(name)
                    bank_free(u, items, i)
                    if name == "C0":
                        pe.wait_ge(kv_done, u + 2)
                        pe.wait_ge(toep_done, u + 2)
                        conv(1 - j, 0, item_bank(i))
                    elif name[0] == "C":
                        conv(j, int(name[1]), item_bank(i))
                    else:
                        if name == "K" and j == 0:
                            pe.wait_ge(x_lo_done, 2)
                        if name in ("K", "Q2") and j == 1:
                            pe.wait_ge(w_lo_done, 2 * v + (3 if name == "K" else 4))
                        project(1 - j, name, item_bank(i))

                def turn(k):
                    t = 4 * u + k
                    pe.wait_ge(norm_done, t + 1)
                    if k:
                        pe.wait_ge(ptcopy_done, t)
                    for h in range(HG):
                        last = pe.transpose(probT_bank[:, h * P:(h + 1) * P],
                                            prob[:, k % 2, h * P:(h + 1) * P], ident[:, :])
                    last.then_inc(pt_done, 1)

                def values(k):
                    t = 4 * u + k
                    if k == 0:
                        pe.wait_ge(v_done, u + 1)
                    pe.wait_ge(ptcopy_done, t + 1)
                    if k:
                        pe.wait_ge(head_lo_done, t)
                    pe.matmul(headT_bank[:, :], v_tok[:, j, k * P:(k + 1) * P], probT[:, k % 2, :],
                              start=True, stop=True).then_inc(pv_done, 1)

                def output(k):
                    t = 4 * u + k
                    if k == 0:
                        pe.wait_ge(wo_lo_done, v + 1)
                    pe.wait_ge(head_lo_done, t + 1)
                    for h in range(HG):
                        for n, (hp, wp) in enumerate(((head_hi, wo_hi), (head_hi, wo_lo),
                                                      (head_lo, wo_hi))):
                            last = pe.matmul(acc_bank[k // 2][:, (k % 2) * D:(k % 2 + 1) * D],
                                             hp[:, k % 2, h * P:(h + 1) * P], wp[:, 4 * v + h, :],
                                             start=(h + n == 0), stop=(h == HG - 1 and n == 2))
                    last.then_inc(wo_done, 1)

                if not has_next:
                    item("C1")
                    turn(0)
                    item("C2")
                    item("C3")
                    scores(u, j, 2)
                    values(0)
                    turn(1)
                    scores(u, j, 3)
                    pe.wait_ge(conv_done, CONV * UNITS)
                    x1_turn(0, 0)
                    output(0)
                    values(1)
                    turn(2)
                    x1_turn(1, 1)
                    output(1)
                    values(2)
                    turn(3)
                    mix_turn(0, 0)
                    output(2)
                    values(3)
                    pe.wait_ge(in_ffn, 64)
                    x2_turn(0, 0)
                    gate_project(0, 0)
                    x1_turn(2, 0)
                    output(3)
                    return

                item("K")
                turn(0)
                item("Q0")
                values(0)
                item("Q1")
                scores(u, j, 2)
                output(0)
                item("Q2")
                turn(1)
                item("Q3")
                values(1)
                item("C1")
                scores(u, j, 3)
                output(1)
                item("C2")
                turn(2)
                item("C3")
                values(2)
                scores(u + 1, 1 - j, 0)
                item("C0")
                turn(3)
                output(2)
                values(3)
                item("V")
                scores(u + 1, 1 - j, 1)
                v_turn(u + 1, item_bank(BODY.index("V")))
                output(3)


            def x1_turn(b, j):
                pe.wait_ge(ln1[4], b + 1)
                if isinstance(b, int) and b == 1:
                    pe.wait_ge(qmix_done, 1)
                else:
                    at_least(pe, x2copy_done, b, 2)
                for c in range(C):
                    last = pe.transpose(mix_bank[:, c * P:(c + 1) * P], x1[:, j, c * P:(c + 1) * P],
                                        ident[:, :])
                last.then_inc(x1T_done, 1)

            def mix_turn(b, j):
                pe.wait_ge(mixT_done, b + 1)
                pe.wait_ge(qmix_done, NB if isinstance(b, int) and b == NB - 1 else b + 2)
                for c in range(C):
                    last = pe.transpose(mix_bank[:, c * P:(c + 1) * P], mixT[:, j, c * P:(c + 1) * P],
                                        ident[:, :])
                last.then_inc(mix_done, 1)

            def x2_turn(b, j):
                pe.wait_ge(ln2[5], b + 1)
                for c in range(C):
                    last = pe.transpose(mix_bank[:, c * P:(c + 1) * P], x2[:, j, c * P:(c + 1) * P],
                                        ident[:, :])
                last.then_inc(x2T_done, 1)

            def gate_project(b, j):
                pe.wait_ge(x2copy_done, b + 1)
                at_least(pe, qf_lo_done, b, 1)
                for c in range(C):
                    last = pe.matmul(tf_bank[:, D:D + FH], x2T[:, j, c * P:(c + 1) * P],
                                     wf[:, c, 3 * D:3 * D + FH], start=(c == 0), stop=(c == C - 1))
                last.then_inc(gate_mm_done, 1)

            def kv_project(b, j, c):
                if c == 0:
                    at_least(pe, masked_done, b, 1)
                last = pe.matmul(kvf_bank[:, :], x2T[:, j, c * P:(c + 1) * P], wf[:, c, D:3 * D],
                                 start=(c == 0), stop=(c == C - 1))
                if c == C - 1:
                    last.then_inc(kvf_done, 1)

            def query_project(b, j):
                if isinstance(b, int) and b == 0:
                    pe.wait_ge(gate_done, 1)
                else:
                    pe.wait_ge(kscopy_done, b + 1)
                for n in range(C):
                    for c in range(C):
                        last = pe.matmul(tf_bank[:, n * P:(n + 1) * P], wf[:, c, n * P:(n + 1) * P],
                                         x2T[:, j, c * P:(c + 1) * P], start=(c == 0), stop=(c == C - 1))
                last.then_inc(qT_done, 1)

            def key_turn(b):
                pe.wait_ge(krep_done, b + 1)
                if isinstance(b, int) and b == 0:
                    pe.wait_ge(qf_lo_done, 1)
                pe.transpose(tf_bank[:, 0:P], krep[:, :, :].rearrange("p n d -> p (n d)"),
                             ident[:, :]).then_inc(ksT_done, 1)

            def fscores(b, j, c):
                if c == 0:
                    pe.wait_ge(kblock_hi_done, b + 1)
                    pe.wait_ge(kblock_lo_done, b + 1)
                    pe.wait_ge(qf_lo_done, b + 1)
                out = fscore_bank[c % 2]
                own = slice(CW * (c % 2), CW * (c % 2 + 1))
                pe.matmul(out[:, :], qf[:, j, c, :], kblock[:, j, 0, :, :], start=True, stop=False)
                pe.matmul(out[:, :], qf[own, j, c, :], kblock[own, j, 1, :, :], start=False, stop=False)
                pe.matmul(out[:, :].rearrange("p (h k) -> p h k", k=P), identb[:, :],
                          causal[:, :].unsqueeze(1).to_broadcast([P, 4, P]),
                          start=False, stop=True).then_inc(fscores_done, 1)

            def fturn(b, c):
                pe.wait_ge(fexp_done, 4 * b + c + 1)
                for h in range(4):
                    last = pe.transpose(fprobT_bank[c % 2][:, h * P:(h + 1) * P],
                                        prob[:, c % 2, h * P:(h + 1) * P], ident[:, :])
                last.then_inc(fpt_done, 1)

            def fvalues(b, c):
                pe.wait_ge(fptcopy_done, 4 * b + c + 1)
                if c == 0:
                    pe.wait_ge(vext_done, b + 1)
                    at_least(pe, ynorm_done, b, 1)
                for h in range(4):
                    f = 4 * c + h
                    last = pe.matmul(y_bank[:, f * (FD + 1):(f + 1) * (FD + 1)],
                                     probT[:, c % 2, h * P:(h + 1) * P], vext[:, b, :],
                                     start=True, stop=True)
                last.then_inc(y_done, 1)

            phase_a(pe, unit)

            pe.wait_ge(acc_done, 2 * UNITS - 1)
            kv_project(0, 0, 0)
            kv_project(0, 0, 1)
            query_project(0, 0)
            mix_turn(1, 1)
            key_turn(0)
            x2_turn(1, 1)
            x1_turn(3, 1)
            gate_project(1, 1)
            pe.wait_ge(mask_done, 1)
            pe.wait_ge(acc_done, 2 * UNITS)
            fscores(0, 0, 0)
            fscores(0, 0, 1)
            kv_project(1, 1, 0)
            kv_project(1, 1, 1)
            fturn(0, 0)
            mix_turn(2, 0)
            fscores(0, 0, 2)
            key_turn(1)

            def seq(b, j):
                query_project(b + 1, 1 - j)
                fturn(b, 1)
                fscores(b, j, 3)
                x2_turn(b + 2, j)
                fvalues(b, 0)
                fturn(b, 2)
                x1_turn(b + 4, j)
                fvalues(b, 1)
                fscores(b + 1, 1 - j, 0)
                gate_project(b + 2, j)
                kv_project(b + 2, j, 0)
                kv_project(b + 2, j, 1)
                fvalues(b, 2)
                fturn(b, 3)
                fscores(b + 1, 1 - j, 1)
                mix_turn(b + 3, 1 - j)
                fturn(b + 1, 0)
                key_turn(b + 2)
                fvalues(b, 3)
                fscores(b + 1, 1 - j, 2)

            def last_seq(b, j):
                if b + 1 < NB:
                    query_project(b + 1, 1 - j)
                fturn(b, 1)
                fscores(b, j, 3)
                if b + 2 < NB:
                    x2_turn(b + 2, j)
                fvalues(b, 0)
                fturn(b, 2)
                if b + 1 < NB:
                    fscores(b + 1, 1 - j, 0)
                if b + 2 < NB:
                    gate_project(b + 2, j)
                fvalues(b, 1)
                fturn(b, 3)
                if b + 1 < NB:
                    fscores(b + 1, 1 - j, 1)
                if b + 2 < NB:
                    kv_project(b + 2, j, 0)
                    kv_project(b + 2, j, 1)
                fvalues(b, 2)
                if b + 3 < NB:
                    mix_turn(b + 3, 1 - j)
                if b + 1 < NB:
                    fturn(b + 1, 0)
                if b + 2 < NB:
                    key_turn(b + 2)
                if b + 1 < NB:
                    fscores(b + 1, 1 - j, 2)
                fvalues(b, 3)

            phase_b(pe, seq, last_seq)

        @block.scalar
        def _(act):
            act.dma_start(w_raw[:, :, 0:3 * P], wqkv_d[:, 0, :, 0:3 * P]).then_inc(in_w_first, 16)
            act.dma_start(w_raw[:, :, 3 * P:], wqkv_d[:, 0, :, 3 * P:]).then_inc(in_w, 16)

            def split_w(g, part, uses):
                if isinstance(g, int) and part == 0:
                    act.wait_ge(in_w_first, 16)
                elif isinstance(g, int) or part == 0:
                    act.wait_ge(in_w, 16 * g + 16)
                if uses is not None:
                    act.wait_ge(proj_done, uses)
                cols = slice(part * 3 * P, (part + 1) * 3 * P)
                act.copy(w_hi[:, :, cols], w_raw[:, :, cols]).then_inc(w_hi_done, 1)

            def split_wo(g):
                act.wait_ge(in_wo, 16 * g + 16)
                act.copy(wo_hi[:, bass.ds(HG * g, HG), :], wo_raw[:, :, :]).then_inc(wo_hi_done, 1)

            act.wait_ge(in_xt, 16)
            act.copy(x_hi[:, 0, :, :], x_raw[:, :, :]).then_inc(x_hi_done, 1)
            split_w(0, 0, None)
            split_w(0, 1, None)

            def rotate(u_next, j_next, name, bank_in, count):
                r, par = rope_count(u_next, name), rope_parity(j_next, name)
                act.wait_ge(proj_done, count)
                if not (isinstance(r, int) and r <= 2):
                    act.wait_ge(sin_done, r - 2)
                H2 = P // 2
                act.copy(rot[0:H2, par, :], bank_in[H2:P, :])
                act.copy(rot[H2:P, par, :], bank_in[0:H2, :]).then_inc(rot_done, 1)

            def copy_vT(bank_in, count):
                act.wait_ge(proj_done, count)
                act.copy(vT[:, :], bank_in[:, :]).then_inc(vT_done, 1)

            def copy_v(u_next, j_next, bank_in):
                act.wait_ge(v_turned, u_next + 1)
                act.copy(v_tok[:, j_next, :], bank_in[:, :]).then_inc(v_done, 1)

            def conv_copy(j, i, h, bank_in, count):
                act.wait_ge(proj_done, count)
                act.copy(y36[:, :, i % 2, h, :],
                         bank_in[:, 0:NB * NPAIR].rearrange("p (b n) -> p b n", b=NB)
                         ).then_inc(conv_done, 1)

            def exps(u, k):
                t = 4 * u + k
                act.wait_ge(max_done, t + 1)
                if not (isinstance(t, int) and t < 2):
                    act.wait_ge(pt_done, t - 1)
                for h in range(HG):
                    last = act.activation(prob[:, k % 2, h * P:(h + 1) * P],
                                          score_bank[k % 2][:, h * P:(h + 1) * P], ACT.Exp,
                                          bias=neg_max[:, k % 2, h:h + 1],
                                          accum_out=den[:, k % 2, h:h + 1])
                last.then_inc(exp_done, 1)

            for n, name in enumerate(ROPED):
                rotate(0, 0, name, front_bank[name], n + 1)
            act.wait_ge(in_xt, 32)
            act.copy(x_hi[:, 1, :, :], x_raw[:, :, :]).then_inc(x_hi_done, 1)
            copy_vT(front_bank["V"], FRONT.index("V") + 1)
            copy_v(0, 0, front_bank["V"])
            exps(0, 0)
            conv_copy(0, 0, 0, front_bank["C0"], FRONT.index("C0") + 1)
            split_wo(0)
            exps(0, 1)

            def unit(v, j, has_next, has_more):
                u = 2 * v + j
                items = BODY if has_next else LAST

                def item(name):
                    if name not in items:
                        return
                    at = items.index(name)
                    if name == "V":
                        copy_vT(item_bank(at), proj_count(u, at))
                    elif name == "C0":
                        conv_copy(1 - j, 0, 4 * v + 2 * j + 2, item_bank(at), proj_count(u, at))
                    elif name[0] == "C":
                        i = int(name[1])
                        conv_copy(j, i, 4 * v + 2 * j + i // 2, item_bank(at), proj_count(u, at))
                    else:
                        rotate(u + 1, j + 1, name, item_bank(at), proj_count(u, at))

                def head_copy(k):
                    t = 4 * u + k
                    act.wait_ge(pv_done, t + 1)
                    two_back(act, wo_done, u, k)
                    act.copy(head_hi[:, k % 2, :], headT_bank[:, :]).then_inc(head_hi_done, 1)

                if not has_next:
                    item("C1")
                    item("C2")
                    item("C3")
                    head_copy(0)
                    exps(u, 2)
                    mix_query(0, 0)
                    exps(u, 3)
                    head_copy(1)
                    mix_query(1, 1)
                    head_copy(2)
                    head_copy(3)
                    return

                item("K")
                item("Q0")
                head_copy(0)
                item("Q1")
                exps(u, 2)
                item("Q2")
                item("Q3")
                head_copy(1)
                item("C1")
                exps(u, 3)
                item("C2")
                if j == 0 and has_more:
                    split_w(v + 1, 0, proj_count(u, BODY.index("Q1")))
                item("C3")
                head_copy(2)
                exps(u + 1, 0)
                item("C0")
                if j == 1:
                    split_wo(v + 1)
                head_copy(3)
                item("V")
                if j == 0 and has_more:
                    split_w(v + 1, 1, proj_count(u, BODY.index("V")))
                copy_v(u + 1, 1 - j, item_bank(BODY.index("V")))
                exps(u + 1, 1)

            def mix_query(b, j):
                act.wait_ge(x1T_done, b + 1)
                at_least(act, prod_done, b, 2)
                act.copy(qmix[:, j, :], mix_bank[:, 0:D]).then_inc(qmix_done, 1)

            def x2_copy(b, j):
                act.wait_ge(x2T_done, b + 1)
                act.copy(x2T[:, j, :], mix_bank[:, 0:D]).then_inc(x2copy_done, 1)

            def keep_x2(b, j):
                act.wait_ge(ln2[5], b + 1)
                act.copy(x[:, b, :], x2[:, j, :]).then_inc(x2_kept, 1)

            def gate_copy(b):
                act.wait_ge(gate_mm_done, b + 1)
                at_least(act, chosen_done, b, 1)
                act.copy(gate[:, :], tf_bank[:, D:D + FH]).then_inc(gate_done, 1)

            def query_hi(b, j):
                act.wait_ge(qT_done, b + 1)
                queries = tf_bank[:, 0:D].rearrange("p (n t) -> p n t", t=P)
                for r in range(2):
                    own = slice(CW * r, CW * (r + 1))
                    last = act.mul(qf[own, j, r::2, :], queries[own, :, :], FD ** -0.5)
                last.then_inc(qf_hi_done, 1)

            def gate_exp(b):
                act.wait_ge(gneg_done, b + 1)
                at_least(act, gprob_done, b, 1)
                act.activation(gexp[:, :], gate[:, :], ACT.Exp, bias=gneg[:, 0:1],
                               accum_out=gsum[:, 0:1]).then_inc(gexp_done, 1)

            def key_copy(b):
                act.wait_ge(ksT_done, b + 1)
                at_least(act, kblock_lo_done, b, 1)
                act.copy(ksT[:, :], tf_bank[:, 0:P])
                act.copy(ksT_hi[:, :], tf_bank[:, 0:P]).then_inc(kscopy_done, 1)

            def block_keys_hi(b, j):
                if isinstance(b, int) and b == 0:
                    act.wait_ge(in_ffn, 64)
                act.wait_ge(kscopy_done, b + 1)
                for c in range(FC):
                    last = act.activation(kblock[:, j, 0, c, :], ksT_hi[:, :].bitcast(FP32), ACT.Copy,
                                          scale=blocks[:, c:c + 1])
                last.then_inc(kblock_hi_done, 1)

            def fexps(b, c):
                act.wait_ge(fmax_done, 4 * b + c + 1)
                for h in range(4):
                    last = act.activation(prob[:, c % 2, h * P:(h + 1) * P],
                                          fscore_bank[c % 2][:, h * P:(h + 1) * P], ACT.Exp,
                                          bias=neg_max[:, c % 2, h:h + 1])
                last.then_inc(fexp_done, 1)

            def fprob_copy(b, c):
                act.wait_ge(fpt_done, 4 * b + c + 1)
                act.copy(probT[:, c % 2, :], fprobT_bank[c % 2][:, :]).then_inc(fptcopy_done, 1)

            phase_a(act, unit)

            x2_copy(0, 0)
            keep_x2(0, 0)
            gate_copy(0)
            mix_query(2, 0)
            gate_exp(0)
            query_hi(0, 0)
            key_copy(0)
            block_keys_hi(0, 0)
            x2_copy(1, 1)
            mix_query(3, 1)
            keep_x2(1, 1)
            gate_copy(1)
            gate_exp(1)
            fexps(0, 0)
            fexps(0, 1)
            fprob_copy(0, 0)
            key_copy(1)
            block_keys_hi(1, 1)

            def seq(b, j):
                query_hi(b + 1, 1 - j)
                fexps(b, 2)
                fprob_copy(b, 1)
                x2_copy(b + 2, j)
                mix_query(b + 4, j)
                keep_x2(b + 2, j)
                fexps(b, 3)
                fprob_copy(b, 2)
                gate_copy(b + 2)
                fexps(b + 1, 0)
                gate_exp(b + 2)
                fprob_copy(b, 3)
                fexps(b + 1, 1)
                key_copy(b + 2)
                fprob_copy(b + 1, 0)
                block_keys_hi(b + 2, j)

            def last_seq(b, j):
                if b + 1 < NB:
                    query_hi(b + 1, 1 - j)
                fexps(b, 2)
                fprob_copy(b, 1)
                if b + 2 < NB:
                    x2_copy(b + 2, j)
                fexps(b, 3)
                fprob_copy(b, 2)
                if b + 2 < NB:
                    gate_copy(b + 2)
                if b + 1 < NB:
                    fexps(b + 1, 0)
                if b + 2 < NB:
                    gate_exp(b + 2)
                    keep_x2(b + 2, j)
                fprob_copy(b, 3)
                if b + 1 < NB:
                    fexps(b + 1, 1)
                if b + 2 < NB:
                    key_copy(b + 2)
                if b + 1 < NB:
                    fprob_copy(b + 1, 0)
                if b + 2 < NB:
                    block_keys_hi(b + 2, j)

            phase_b(act, seq, last_seq)

        @block.vector
        def _(dve):
            def take_cos(u_next, j_next, name, bank_in):
                r, par = rope_count(u_next, name), rope_parity(j_next, name)
                dve.wait_ge(rot_done, r)
                if not (isinstance(r, int) and r <= 2):
                    dve.wait_ge(rope_done, r - 2)
                dve.tensor_tensor(t_cos[:, par, :].rearrange("p (b t) -> p b t", b=BH),
                                  bank_in[:, :].rearrange("p (b t) -> p b t", b=BH),
                                  cos[:, :].unsqueeze(1).to_broadcast([P, BH, P]),
                                  ALU.mult).then_inc(cos_done, 1)

            def add_sin(u_next, j_next, name):
                r, par = rope_count(u_next, name), rope_parity(j_next, name)
                if name == "K":
                    dst = k_rope[:, j_next % 2, :]
                else:
                    dst = q_rope[:, j_next % 2, int(name[1]), :]
                dve.wait_ge(cos_done, r)
                dve.wait_ge(sin_done, r)
                dve.tensor_tensor(dst, t_cos[:, par, :], t_sin[:, par, :], ALU.add
                                  ).then_inc(rope_done, 1)

            dve.memset(half_pow[:, :], -0.5)
            dve.memset(vext[:, :, FD:FD + 1], 1.0).then_inc(const_set, 1)

            def split_lo(lo, raw, hi, hi_ready, count, done):
                dve.wait_ge(hi_ready, count)
                dve.tensor_tensor(lo, raw, hi.bitcast(FP32), ALU.subtract).then_inc(done, 1)

            def split_w(g, part):
                cols = slice(part * 3 * P, (part + 1) * 3 * P)
                split_lo(w_lo[:, :, cols], w_raw[:, :, cols], w_hi[:, :, cols], w_hi_done,
                         2 * g + part + 1, w_lo_done)

            def add_skip(u, j):
                dve.wait_ge(in_toep[j], 8 * (u - j) + 16)
                for hh in range(2):
                    last = dve.scalar_tensor_tensor(toep[:, j, hh, 0:P], anti[:, :],
                                                    dcoef[:, bass.ds(2 * u + hh, 1)],
                                                    toep[:, j, hh, 0:P], ALU.mult, ALU.add)
                last.then_inc(toep_done, 1)

            split_lo(x_lo[:, 0, :, :], x_raw[:, :, :], x_hi[:, 0, :, :], x_hi_done, 1, x_lo_done)
            split_w(0, 0)
            split_w(0, 1)
            dve.wait_ge(in_skip, 32)
            add_skip(0, 0)
            dve.wait_ge(in_trig, 32)
            for n, name in enumerate(ROPED):
                take_cos(0, 0, name, front_bank[name])
                if n >= 1:
                    add_sin(0, 0, ROPED[n - 1])
            add_sin(0, 0, ROPED[-1])

            def row_max(u, k):
                t = 4 * u + k
                dve.wait_ge(scores_done, t + 1)
                dve.tensor_reduce(neg_max[:, k % 2, :],
                                  score_bank[k % 2][:, :].rearrange("p (h k) -> p h k", h=HG),
                                  axis=AX.X, op=ALU.max, negate=True).then_inc(max_done, 1)

            def invert(u, k):
                t = 4 * u + k
                dve.wait_ge(exp_done, t + 1)
                dve.reciprocal(rden[:, k % 2, :], den[:, k % 2, :]).then_inc(rden_done, 1)

            split_lo(x_lo[:, 1, :, :], x_raw[:, :, :], x_hi[:, 1, :, :], x_hi_done, 2, x_lo_done)
            row_max(0, 0)
            row_max(0, 1)
            invert(0, 0)
            invert(0, 1)

            def unit(v, j, has_next, has_more):
                u = 2 * v + j

                def cos_item(name):
                    take_cos(u + 1, j + 1, name, item_bank(BODY.index(name)))

                def add_item(name):
                    add_sin(u + 1, j + 1, name)

                def prob_copy(k):
                    t = 4 * u + k
                    dve.wait_ge(pt_done, t + 1)
                    two_back(dve, pv_done, u, k)
                    dve.tensor_copy(probT[:, k % 2, :], probT_bank[:, :]).then_inc(ptcopy_done, 1)

                def head_low(k):
                    t = 4 * u + k
                    dve.wait_ge(head_hi_done, t + 1)
                    dve.tensor_tensor(head_lo[:, k % 2, :], headT_bank[:, :],
                                      head_hi[:, k % 2, :].bitcast(FP32), ALU.subtract
                                      ).then_inc(head_lo_done, 1)

                def accumulate(a):
                    dve.wait_ge(wo_done, 4 * u + 2 * a + 2)
                    if a == 0:
                        dve.wait_ge(in_x, 16)
                    own = x[:, j * BH + 2 * a:j * BH + 2 * a + 2, :]
                    dve.tensor_tensor(own, acc_bank[a][:, :].rearrange("p (b n) -> p b n", b=2), own,
                                      ALU.add).then_inc(acc_done, 1)

                if not has_next:
                    first_stats(0)
                    prob_copy(0)
                    row_max(u, 2)
                    first_apply(0, 0)
                    prob_copy(1)
                    head_low(0)
                    row_max(u, 3)
                    invert(u, 2)
                    dve.wait_ge(conv_done, CONV * UNITS)
                    dve.wait_ge(qmix_done, 1)
                    pair_products(dve, 0, 0, NEAR).then_inc(near_done, 1)
                    invert(u, 3)
                    dve.wait_ge(pv_done, 4 * u + 2)
                    first_apply(1, 1)
                    head_low(1)
                    prob_copy(2)
                    dve.wait_ge(near_done, 1)
                    mix_sum(0, 0)
                    prob_copy(3)
                    head_low(2)
                    add_mix(0, 0)
                    norm_stats(0, ln2, 0, x1[:, 0, :])
                    norm_aggr(0, ln2, 0)
                    norm_eps(0, ln2, 0)
                    accumulate(0)
                    dve.wait_ge(in_ffn, 64)
                    dve.tensor_copy(causal[:, :], causal_raw[:, :])
                    dve.tensor_copy(identb[:, :], ident[:, :]).then_inc(mask_done, 1)
                    second_apply(0, 0)
                    first_apply(2, 0)
                    head_low(3)
                    gating(0)
                    accumulate(1)
                    return

                prob_copy(0)
                cos_item("K")
                add_item("K")
                head_low(0)
                cos_item("Q0")
                add_item("Q0")
                row_max(u, 2)
                cos_item("Q1")
                add_item("Q1")
                invert(u, 2)
                prob_copy(1)
                add_skip(u + 1, 1 - j)
                cos_item("Q2")
                add_item("Q2")
                head_low(1)
                cos_item("Q3")
                add_item("Q3")
                row_max(u, 3)
                accumulate(0)
                prob_copy(2)
                invert(u, 3)
                if j == 0 and has_more:
                    split_w(v + 1, 0)
                head_low(2)
                row_max(u + 1, 0)
                prob_copy(3)
                invert(u + 1, 0)
                head_low(3)
                if j == 0 and has_more:
                    split_w(v + 1, 1)
                row_max(u + 1, 1)
                accumulate(1)
                invert(u + 1, 1)

            def first_stats(s):
                dve.wait_ge(acc_done, 2 * (UNITS - 1 + s))
                for i in range(BH):
                    last = dve.bn_stats(stats[:, i, :], x[:, s * BH + i, :])
                last.then_inc(ln1[0], 1)
                dve.wait_ge(ln1[0], s + 1)
                for i in range(BH):
                    last = dve.bn_aggr(mean_var1[:, s * BH + i, :], stats[:, i, :])
                last.then_inc(ln1[1], 1)
                dve.wait_ge(ln1[1], s + 1)
                dve.tensor_scalar(var_eps1[:, s * BH:(s + 1) * BH], mean_var1[:, s * BH:(s + 1) * BH, 1],
                                  EPS, None, ALU.add).then_inc(ln1[2], 1)

            def first_apply(b, j):
                dve.wait_ge(ln1[3], b // BH + 1 if isinstance(b, int) else NS)
                at_least(dve, ln2[5], b, 2)
                dve.tensor_scalar(x1[:, j, :], x[:, b, :], mean_var1[:, b, 0:1], rstd1[:, bass.ds(b, 1)],
                                  ALU.subtract, ALU.mult).then_inc(ln1[4], 1)

            def norm_stats(n, ln, b, src):
                dve.wait_ge(ln[0], b + 1)
                dve.bn_stats(stats_of[n][:, :], src).then_inc(ln[1], 1)

            def norm_aggr(n, ln, b):
                dve.wait_ge(ln[1], b + 1)
                dve.memset(carrier[:, :], 0.0)
                dve.bn_aggr(mean_var_of[n][:, :], stats_of[n][:, :]).then_inc(ln[2], 1)

            def norm_eps(n, ln, b):
                dve.wait_ge(ln[2], b + 1)
                dve.tensor_scalar(var_eps_of[n][:, :], mean_var_of[n][:, 1:2], EPS, None, ALU.add
                                  ).then_inc(ln[3], 1)

            def norm_apply(n, ln, b, src, out):
                dve.wait_ge(ln[4], b + 1)
                dve.tensor_scalar(out, src, mean_var_of[n][:, 0:1], rstd_of[n][:, 0:1],
                                  ALU.subtract, ALU.mult).then_inc(ln[5], 1)

            def second_apply(b, j):
                at_least(dve, x2_kept, b, 2)
                norm_apply(0, ln2, b, x1[:, j, :], x2[:, j, :])

            def mix_sum(b, j):
                dve.wait_ge(prod_done, b + 1)
                at_least(dve, mix_done, b, 2)
                dve.tensor_reduce(mixT[:, j, :], prod[:, j, :, :, :], axis=AX.X, op=ALU.add
                                  ).then_inc(mixT_done, 1)

            def add_mix(b, j):
                dve.wait_ge(mix_done, b + 1)
                dve.wait_ge(ln1[4], b + 1)
                dve.tensor_tensor(x1[:, j, :], mix_bank[:, 0:D], x1[:, j, :], ALU.add).then_inc(ln2[0], 1)

            def mix_norm(b, j):
                add_mix(b, j)
                norm_stats(0, ln2, b, x1[:, j, :])
                norm_aggr(0, ln2, b)
                norm_eps(0, ln2, b)
                second_apply(b, j)

            def gating(b):
                dve.wait_ge(gate_done, b + 1)
                at_least(dve, gexp_done, b, 1)
                dve.tensor_reduce(gtop[:, 0:1], gate[:, :], axis=AX.X, op=ALU.max).then_inc(gtop_done, 1)
                dve.tensor_reduce(gneg[:, 0:1], gate[:, :], axis=AX.X, op=ALU.max, negate=True
                                  ).then_inc(gneg_done, 1)
                dve.wait_ge(gtop_done, b + 1)
                dve.scalar_tensor_tensor(gscore[:, :], gate[:, :], gtop[:, 0:1], ties[:, :],
                                         ALU.is_equal, ALU.mult).then_inc(gscore_done, 1)
                dve.wait_ge(gscore_done, b + 1)
                dve.tensor_reduce(gbest[:, 0:1], gscore[:, :], axis=AX.X, op=ALU.max
                                  ).then_inc(gbest_done, 1)
                dve.wait_ge(gbest_done, b + 1)
                dve.tensor_scalar(chosen[:, :], gscore[:, :], gbest[:, 0:1], None, ALU.is_equal
                                  ).then_inc(chosen_done, 1)

            def query_lo(b, j):
                dve.wait_ge(qf_hi_done, b + 1)
                queries = tf_bank[:, 0:D].rearrange("p (n t) -> p n t", t=P)
                for r in range(2):
                    own, other = slice(CW * r, CW * (r + 1)), slice(CW * (1 - r), CW * (2 - r))
                    last = dve.scalar_tensor_tensor(qf[other, j, r::2, :], queries[own, :, :], FD ** -0.5,
                                                    qf[own, j, r::2, :].bitcast(FP32),
                                                    ALU.mult, ALU.subtract)
                last.then_inc(qf_lo_done, 1)

            def share(b):
                dve.wait_ge(chosen_done, b + 1)
                dve.wait_ge(kvf_done, b + 1)
                dve.tensor_tensor(kv_masked[:, :, :, :],
                                  kvf_bank[:, :].rearrange("p (n h d) -> p n h d", n=2, h=FH),
                                  chosen[:, :].unsqueeze(1).unsqueeze(3).to_broadcast([P, 2, FH, FD]),
                                  ALU.mult).then_inc(masked_done, 1)
                dve.wait_ge(gexp_done, b + 1)
                dve.reciprocal(gprob[:, 0:1], gsum[:, 0:1]).then_inc(gprob_done, 1)
                dve.wait_ge(masked_done, b + 1)
                dve.tensor_reduce(kv_shared[:, :, :],
                                  kv_masked[:, :, :, :].rearrange("p n h d -> p n d h"),
                                  axis=AX.X, op=ALU.add).then_inc(shared_done, 1)
                dve.wait_ge(shared_done, b + 1)
                at_least(dve, ksT_done, b, 1)
                dve.tensor_copy(krep[:, :, :], kv_shared[:, 0, :].unsqueeze(1).to_broadcast([P, FB, FD])
                                ).then_inc(krep_done, 1)
                dve.wait_ge(gprob_done, b + 1)
                dve.tensor_scalar(vext[:, b, 0:FD], kv_shared[:, 1, :], gprob[:, 0:1], None, ALU.mult
                                  ).then_inc(vext_done, 1)

            def frow_max(b, c):
                dve.wait_ge(fscores_done, 4 * b + c + 1)
                dve.tensor_reduce(neg_max[:, c % 2, :],
                                  fscore_bank[c % 2][:, :].rearrange("p (h k) -> p h k", h=4),
                                  axis=AX.X, op=ALU.max, negate=True).then_inc(fmax_done, 1)

            y = y_bank[:, 0:FH * (FD + 1)].rearrange("p (h d) -> p h d", h=FH)

            y_flat = ynorm[:, :, :].rearrange("p h d -> p (h d)")

            def y_invert(b):
                dve.wait_ge(y_done, 4 * b + 4)
                dve.reciprocal(yden[:, :], y[:, :, FD]).then_inc(yden_done, 1)

            def y_scale(b):
                dve.wait_ge(yden_done, b + 1)
                dve.tensor_tensor(ynorm[:, :, :], y[:, :, 0:FD],
                                  yden[:, :].unsqueeze(2).to_broadcast([P, FH, FD]), ALU.mult
                                  ).then_inc(ynorm_done, 1)

            def add_ffn(b):
                dve.wait_ge(ynorm_done, b + 1)
                dve.wait_ge(x2_kept, b + 1)
                dve.tensor_tensor(y_flat, y_flat, x[:, b, :],
                                  ALU.add).then_inc(ln3[0], 1)

            phase_a(dve, unit)

            mix_sum(1, 1)
            query_lo(0, 0)
            add_mix(1, 1)
            norm_stats(0, ln2, 1, x1[:, 1, :])
            norm_aggr(0, ln2, 1)
            norm_eps(0, ln2, 1)
            share(0)
            second_apply(1, 1)
            first_apply(3, 1)
            first_stats(1)
            gating(1)
            frow_max(0, 0)
            frow_max(0, 1)
            mix_sum(2, 0)
            share(1)
            mix_norm(2, 0)
            frow_max(0, 2)
            query_lo(1, 1)

            def seq(b, j):
                first_apply(b + 4, j)
                frow_max(b, 3)
                mix_sum(b + 3, 1 - j)
                frow_max(b + 1, 0)
                gating(b + 2)
                share(b + 2)
                frow_max(b + 1, 1)
                add_mix(b + 3, 1 - j)
                norm_stats(0, ln2, b + 3, x1[:, 1 - j, :])
                y_invert(b)
                norm_aggr(0, ln2, b + 3)
                y_scale(b)
                norm_eps(0, ln2, b + 3)
                add_ffn(b)
                norm_stats(1, ln3, b, y_flat)
                frow_max(b + 1, 2)
                norm_aggr(1, ln3, b)
                second_apply(b + 3, 1 - j)
                norm_eps(1, ln3, b)
                query_lo(b + 2, j)
                norm_apply(1, ln3, b, y_flat, x[:, b, :])

            def last_seq(b, j):
                frow_max(b, 3)
                if b > NB - 4:
                    norm_apply(1, ln3, b - 1, y_flat, x[:, b - 1, :])
                if b + 1 < NB:
                    frow_max(b + 1, 0)
                if b + 3 < NB:
                    mix_sum(b + 3, 1 - j)
                if b + 2 < NB:
                    gating(b + 2)
                if b + 1 < NB:
                    frow_max(b + 1, 1)
                if b + 2 < NB:
                    share(b + 2)
                if b + 3 < NB:
                    add_mix(b + 3, 1 - j)
                    norm_stats(0, ln2, b + 3, x1[:, 1 - j, :])
                if b + 1 < NB:
                    frow_max(b + 1, 2)
                y_invert(b)
                if b + 3 < NB:
                    norm_aggr(0, ln2, b + 3)
                y_scale(b)
                if b + 3 < NB:
                    norm_eps(0, ln2, b + 3)
                add_ffn(b)
                norm_stats(1, ln3, b, y_flat)
                norm_aggr(1, ln3, b)
                if b + 3 < NB:
                    second_apply(b + 3, 1 - j)
                norm_eps(1, ln3, b)
                if b + 2 < NB:
                    query_lo(b + 2, j)

            phase_b(dve, seq, last_seq)
            norm_apply(1, ln3, NB - 1, y_flat, x[:, NB - 1, :])

        @block.gpsimd
        def _(pool):
            def pairs(u_next, head, buf, distances=range(HD)):
                if not (isinstance(u_next, int) and u_next <= 1):
                    pool.wait_ge(proj_done, proj_count(u_next - 2, BODY.index("C3")))
                src = ctxT[:, :, bass.ds(head * NB, 2 * NB), :]
                for d in distances:
                    at, n = PAIR_AT[d], HD - d
                    last = pool.tensor_tensor(kv[:, buf, :, :, at:at + n], src[:, :, :, 0:n],
                                              src[:, :, :, d:HD], ALU.mult)
                if distances[-1] == HD - 1:
                    last.then_inc(kv_done, 1)

            def times_sin(u_next, j_next, name):
                r, par = rope_count(u_next, name), rope_parity(j_next, name)
                pool.wait_ge(rot_done, r)
                if not (isinstance(r, int) and r <= 2):
                    pool.wait_ge(rope_done, r - 2)
                pool.tensor_tensor(t_sin[:, par, :].rearrange("p (b t) -> p b t", b=BH),
                                   rot[:, par, :].rearrange("p (b t) -> p b t", b=BH),
                                   sin[:, :].unsqueeze(1).to_broadcast([P, BH, P]), ALU.mult
                                   ).then_inc(sin_done, 1)

            pool.wait_ge(in_trig, 32)
            for name in ROPED:
                times_sin(0, 0, name)
            pool.wait_ge(in_ctx, 16)
            pairs(0, 0, 0)

            def split_wo(g):
                pool.wait_ge(wo_hi_done, g + 1)
                heads = bass.ds(HG * g, HG)
                pool.tensor_tensor(wo_lo[:, heads, :], wo_raw[:, :, :], wo_hi[:, heads, :].bitcast(FP32),
                                   ALU.subtract).then_inc(wo_lo_done, 1)

            def normalize(u, k):
                pool.wait_ge(rden_done, 4 * u + k + 1)
                own = prob[:, k % 2, :].rearrange("p (h k) -> p h k", h=HG)
                pool.tensor_tensor(own, own, rden[:, k % 2, :].unsqueeze(2).to_broadcast([P, HG, P]),
                                   ALU.mult).then_inc(norm_done, 1)

            normalize(0, 0)
            split_wo(0)
            normalize(0, 1)

            def unit(v, j, has_next, has_more):
                u = 2 * v + j

                def sin_item(name):
                    times_sin(u + 1, j + 1, name)

                if not has_next:
                    pool.wait_ge(const_set, 1)
                    power(rstd1[:, 0:BH], var_eps1[:, 0:BH], ln1, 1)
                    pool.wait_ge(conv_done, CONV * UNITS)
                    normalize(u, 2)
                    pool.wait_ge(qmix_done, 1)
                    products(0, 0, FAR)
                    normalize(u, 3)
                    return

                sin_item("K")
                sin_item("Q0")
                sin_item("Q1")
                normalize(u, 2)
                sin_item("Q2")
                sin_item("Q3")
                pairs(u + 1, 4 * v + 2 * j + 2, 1 - j)
                normalize(u, 3)
                normalize(u + 1, 0)
                if j == 1:
                    split_wo(v + 1)
                normalize(u + 1, 1)

            def second_power(b):
                power(rstd_of[0][:, :], var_eps_of[0][:, :], ln2, b + 1)

            def products(b, j, distances):
                if distances[0] == 0:
                    pool.wait_ge(qmix_done, b + 1)
                    at_least(pool, mixT_done, b, 2)
                last = pair_products(pool, b, j, distances)
                if distances[-1] == HD - 1:
                    last.then_inc(prod_done, 1)

            def block_keys(b, j):
                mask = blocks[:, :].unsqueeze(2).to_broadcast([P, FC, P])
                pool.wait_ge(kscopy_done, b + 1)
                pool.tensor_tensor(ksT_lo[:, :], ksT[:, :], ksT_hi[:, :].bitcast(FP32), ALU.subtract
                                   ).then_inc(ks_lo_done, 1)
                pool.wait_ge(ks_lo_done, b + 1)
                pool.tensor_tensor(kblock[:, j, 1, :, :],
                                   ksT_lo[:, :].bitcast(FP32).unsqueeze(1).to_broadcast([P, FC, P]),
                                   mask, ALU.mult).then_inc(kblock_lo_done, 1)

            def power(dst, src, ln, count):
                pool.wait_ge(ln[-3], count)
                pool.tensor_tensor(dst, src, half_pow[:, 0:dst.shape[1]], ALU.pow).then_inc(ln[-2], 1)

            phase_a(pool, unit)

            products(1, 1, NEAR)
            second_power(0)
            products(1, 1, FAR)
            products(2, 0, NEAR)
            pool.wait_ge(in_ffn, 64)
            second_power(1)
            block_keys(0, 0)
            products(2, 0, FAR)
            products(3, 1, NEAR)
            power(rstd1[:, BH:NB], var_eps1[:, BH:NB], ln1, 2)
            products(3, 1, FAR)
            second_power(2)
            block_keys(1, 1)

            def seq(b, j):
                products(b + 4, j, NEAR)
                products(b + 4, j, FAR)
                second_power(b + 3)
                block_keys(b + 2, j)
                power(rstd_of[1][:, :], var_eps_of[1][:, :], ln3, b + 1)

            def last_seq(b, j):
                if b + 3 < NB:
                    second_power(b + 3)
                if b + 2 < NB:
                    block_keys(b + 2, j)
                power(rstd_of[1][:, :], var_eps_of[1][:, :], ln3, b + 1)

            phase_b(pool, seq, last_seq)


def _layouts(a):
    import numpy as np
    f = np.float32
    x = np.asarray(a["x"]).reshape(NB * P, D)
    L = {}
    L["xt"] = x.T.reshape(C, P, NS, TOK).transpose(1, 2, 0, 3)
    L["x"] = x.reshape(NB, P, D).transpose(1, 0, 2)
    wq = np.asarray(a["L0_attn_Wq"]).reshape(NG, HG * P, D)
    wk = np.asarray(a["L0_attn_Wk"]).reshape(NG, P, D)
    wv = np.asarray(a["L0_attn_Wv"]).reshape(NG, P, D)
    w = np.concatenate([wk, wq, wv], axis=1)
    L["wqkv"] = w.transpose(0, 2, 1).reshape(NG, C, P, 6 * P).transpose(2, 0, 1, 3)
    L["wo"] = np.asarray(a["L0_attn_Wo"]).T.reshape(NH, P, D).transpose(1, 0, 2)
    filt = np.asarray(a["L0_xattn_ssm_kernel"])
    padded = np.concatenate([np.zeros((XH, P - 1), f), filt], axis=1)
    L["toep"] = np.stack([padded[:, p:p + D] for p in range(P)])
    L["dcoef"] = np.broadcast_to(np.asarray(a["L0_xattn_D"])[None, :], (P, XH))
    c = np.asarray(a["ctx_2048"]).reshape(NB, XH, HD, C, P)[..., ::-1]
    L["ctx"] = c.transpose(4, 3, 1, 0, 2).reshape(P, C, XH * NB, HD)
    wf = np.concatenate([np.asarray(a["L0_ffn_W_qkv"]), np.asarray(a["L0_ffn_W_gate"])], axis=0)
    L["wf"] = wf.T.reshape(C, P, 3 * D + FH).transpose(1, 0, 2)
    inv = (f(1.0) / f(10000.0) ** (np.arange(0, P, 2, dtype=f) / f(P))).astype(f)
    angle = np.repeat(np.arange(P, dtype=f)[:, None] * inv[None, :], 2, axis=1).T
    root = float(P) ** -0.25
    sign = np.where(np.arange(P) < P // 2, -1.0, 1.0)[:, None]
    L["cos"] = (np.cos(angle).astype(np.float64) * root).astype(f)
    L["sin"] = (np.sin(angle).astype(np.float64) * root * sign).astype(f)
    L["ident"] = np.eye(P, dtype=f)
    L["anti"] = np.eye(P, dtype=f)[::-1]
    L["causal"] = np.where(np.tril(np.ones((P, P))) > 0, 0.0, -1e30).astype(f)
    L["blocks"] = (np.arange(P)[:, None] % CW // FD == np.arange(FC)[None, :]).astype(f)
    L["ties"] = np.broadcast_to(np.arange(FH, 0, -1).astype(f)[None, :], (P, FH))
    return {k: np.ascontiguousarray(v) for k, v in L.items()}


def kernel(**inputs):
    import concourse.bacc as bacc
    from concourse.bass_utils import run_bass_kernel_spmd
    nc = bacc.Bacc("TRN2", target_bir_lowering=False, num_devices=1)
    arrays, args = {}, []
    for name, a in _layouts(inputs).items():
        arrays[f"in_{name}"] = a
        args.append(nc.dram_tensor(f"in_{name}", a.shape, mybir.dt.from_np(a.dtype),
                                   kind="ExternalInput").ap())
    out = nc.dram_tensor("out", (NB, P, D), FP32, kind="ExternalOutput").ap()
    decoder_kernel(nc, *args, out)
    result = run_bass_kernel_spmd(nc, [arrays], core_ids=[0])
    return result.results[0]["out"]
```
